# Optimizing a Trainium2 kernel written in Bass

```python
import numpy as np
import jax
import jax.numpy as jnp

def _softmax(x, axis=-1):
    return jax.nn.softmax(x, axis=axis)

def _gelu(x):
    return jax.nn.gelu(x, approximate=True)

def _silu(x):
    return jax.nn.silu(x)

def _sigmoid(x):
    return jax.nn.sigmoid(x)

def _layernorm(x, axis=-1, eps=1e-05):
    m = jnp.mean(x, axis=axis, keepdims=True)
    v = jnp.var(x, axis=axis, keepdims=True)
    return (x - m) / jnp.sqrt(v + eps)

def _scatter_add(tgt, idx, src, axis=0):
    return tgt.at[idx].add(src)

def _segment_sum(src, seg, n):
    return jax.ops.segment_sum(src, seg, n)
kernel_name = 'mk_vit_tower_cls_d1_tok_img1024_r4_a092cb'

def setup_inputs(seed: int=0):
    np.random.seed(seed)
    _w = jnp.asarray

    def _rec_inputs():
        import jax
        import jax.numpy as jnp
        _rk = jax.random.key(seed)
        x = -0.00016672 + 0.999947 * jax.random.normal(jax.random.fold_in(_rk, 1), (16, 3, 96, 96), jnp.float32)
        cls_tok = 0.02 * jax.random.normal(jax.random.fold_in(_rk, 5), (1, 1, 256), jnp.float32)
        return (x, cls_tok)
    x, cls_tok = _rec_inputs()

    def _L0_tok_setup():
        import jax, jax.numpy as jnp
        import numpy as np
        IMG = 96
        PATCH = 16
        C_IN = 3
        EMBED = 256
        NPH = IMG // PATCH
        NUM_PATCHES = NPH * NPH
        PATCH_DIM = PATCH * PATCH * C_IN
        key = jax.random.key(seed)
        k_x, k_w, k_b, k_cls, k_pos = jax.random.split(key, 5)
        x = jax.random.normal(k_x, (64, C_IN, IMG, IMG), dtype=jnp.float32)
        W = jax.random.normal(k_w, (EMBED, PATCH_DIM), dtype=jnp.float32) * (1.0 / np.sqrt(PATCH_DIM))
        b = jax.random.normal(k_b, (EMBED,), dtype=jnp.float32) * 0.01
        cls_token = jax.random.normal(k_cls, (1, 1, EMBED), dtype=jnp.float32) * 0.02
        pos_embed = jax.random.normal(k_pos, (1, NUM_PATCHES + 1, EMBED), dtype=jnp.float32) * 0.02
        return {'x': x, 'W': W, 'b': b, 'cls_token': cls_token, 'pos_embed': pos_embed}
    _L0_tok_all = _L0_tok_setup()
    _L0_tok_in = {k: v for k, v in _L0_tok_all.items() if k in ('W', 'b', 'cls_token', 'pos_embed')}
    del _L0_tok_all

    def _L0_attn_setup():
        import jax, jax.numpy as jnp
        import numpy as np
        D_K, D_MODEL, NUM_HEADS = (64, 256, 16)

        def _xavier(key, shape):
            fan_in, fan_out = (shape[-2], shape[-1])
            limit = float(np.sqrt(6.0 / (fan_in + fan_out)))
            return jax.random.uniform(key, shape, jnp.float32, -limit, limit)
        key = jax.random.key(seed)
        kx, kq, kk, kv, ko = jax.random.split(key, 5)
        x = jax.random.normal(kx, (2, 512, D_MODEL), dtype=jnp.float32)
        w_q = _xavier(kq, (NUM_HEADS, D_MODEL, D_K))
        w_k = _xavier(kk, (NUM_HEADS, D_MODEL, D_K))
        w_v = _xavier(kv, (NUM_HEADS, D_MODEL, D_K))
        w_o = _xavier(ko, (NUM_HEADS * D_K, D_MODEL))
        return {'x': x, 'w_q': w_q, 'w_k': w_k, 'w_v': w_v, 'w_o': w_o}
    _L0_attn_all = _L0_attn_setup()
    _L0_attn_in = {k: v for k, v in _L0_attn_all.items() if k in ('w_q', 'w_k', 'w_v', 'w_o')}
    del _L0_attn_all

    def _L0_ffn_setup():
        import jax, jax.numpy as jnp
        import numpy as np
        E = 8
        K = 2
        CAP_FACTOR = 1.0
        key = jax.random.key(seed)
        ks = jax.random.split(key, 5)
        B, T, C, H = (4, 512, 256, 1024)
        x = jax.random.normal(ks[0], (B, T, C), dtype=jnp.float32)
        Wr = jax.random.normal(ks[1], (C, E), dtype=jnp.float32) * 0.02
        br = jnp.zeros((E,), jnp.float32)
        W1 = jax.random.normal(ks[2], (E, C, H), dtype=jnp.float32) * 0.02
        b1 = jnp.zeros((E, H), jnp.float32)
        W2 = jax.random.normal(ks[3], (E, H, C), dtype=jnp.float32) * 0.02
        b2 = jnp.zeros((E, C), jnp.float32)
        return {'x': x, 'Wr': Wr, 'br': br, 'W1': W1, 'b1': b1, 'W2': W2, 'b2': b2}
    _L0_ffn_all = _L0_ffn_setup()
    _L0_ffn_in = {k: v for k, v in _L0_ffn_all.items() if k in ('Wr', 'br', 'W1', 'b1', 'W2', 'b2')}
    del _L0_ffn_all
    return {'x': x, 'cls_tok': cls_tok, 'L0_tok_W': _L0_tok_in['W'], 'L0_tok_b': _L0_tok_in['b'], 'L0_tok_cls_token': _L0_tok_in['cls_token'], 'L0_tok_pos_embed': _L0_tok_in['pos_embed'], 'L0_attn_w_q': _L0_attn_in['w_q'], 'L0_attn_w_k': _L0_attn_in['w_k'], 'L0_attn_w_v': _L0_attn_in['w_v'], 'L0_attn_w_o': _L0_attn_in['w_o'], 'L0_ffn_Wr': _L0_ffn_in['Wr'], 'L0_ffn_br': _L0_ffn_in['br'], 'L0_ffn_W1': _L0_ffn_in['W1'], 'L0_ffn_b1': _L0_ffn_in['b1'], 'L0_ffn_W2': _L0_ffn_in['W2'], 'L0_ffn_b2': _L0_ffn_in['b2']}

def reference(x, cls_tok, L0_tok_W, L0_tok_b, L0_tok_cls_token, L0_tok_pos_embed, L0_attn_w_q, L0_attn_w_k, L0_attn_w_v, L0_attn_w_o, L0_ffn_Wr, L0_ffn_br, L0_ffn_W1, L0_ffn_b1, L0_ffn_W2, L0_ffn_b2):
    import jax
    import jax.numpy as jnp

    def _L0_tok_ref(x, W, b, cls_token, pos_embed):
        import jax, jax.numpy as jnp
        import numpy as np
        IMG = 96
        PATCH = 16
        C_IN = 3
        EMBED = 256
        NPH = IMG // PATCH
        NUM_PATCHES = NPH * NPH
        PATCH_DIM = PATCH * PATCH * C_IN
        B, C, H, Wd = x.shape
        nph, npw = (H // PATCH, Wd // PATCH)
        patches = x.reshape(B, C, nph, PATCH, npw, PATCH)
        patches = patches.transpose(0, 2, 4, 1, 3, 5)
        patches = patches.reshape(B, nph * npw, C * PATCH * PATCH)
        proj = jnp.einsum('bnd,ed->bne', patches, W) + b
        cls = jnp.broadcast_to(cls_token, (B, 1, cls_token.shape[-1]))
        out = jnp.concatenate([cls, proj], axis=1) + pos_embed
        return out

    def _L0_attn_ref(x, w_q, w_k, w_v, w_o):
        import jax, jax.numpy as jnp
        import numpy as np
        D_K, D_MODEL, NUM_HEADS = (64, 256, 16)

        def _xavier(key, shape):
            fan_in, fan_out = (shape[-2], shape[-1])
            limit = float(np.sqrt(6.0 / (fan_in + fan_out)))
            return jax.random.uniform(key, shape, jnp.float32, -limit, limit)
        scale = 1.0 / jnp.sqrt(jnp.asarray(D_K, dtype=jnp.float32))
        q = jnp.einsum('bsd,hdk->bhsk', x, w_q)
        k = jnp.einsum('bsd,hdk->bhsk', x, w_k)
        v = jnp.einsum('bsd,hdk->bhsk', x, w_v)
        scores = jnp.einsum('bhqk,bhmk->bhqm', q, k) * scale
        weights = jax.nn.softmax(scores, axis=-1)
        z = jnp.einsum('bhqm,bhmk->bhqk', weights, v)
        b, h, s, dk = z.shape
        z = jnp.transpose(z, (0, 2, 1, 3)).reshape(b, s, h * dk)
        z = jnp.einsum('bse,ed->bsd', z, w_o)
        return x + z

    def _L0_ffn_ref(x, Wr, br, W1, b1, W2, b2):
        import jax, jax.numpy as jnp
        import numpy as np
        E = 8
        K = 2
        CAP_FACTOR = 1.0
        B, T, C = x.shape
        N = B * T
        xf = x.reshape(N, C)
        logits = xf @ Wr + br
        topv, topi = jax.lax.top_k(logits, K)
        gates = jax.nn.softmax(topv, axis=-1)
        rw = jnp.zeros((N, E), xf.dtype).at[jnp.arange(N)[:, None], topi].set(gates)
        cap = int(N * K / E * CAP_FACTOR)
        sel = jax.nn.one_hot(topi, E, dtype=jnp.int32).sum(1)
        rank = jnp.cumsum(sel, axis=0) - sel
        keep = (sel > 0) & (rank < cap)
        tok = jnp.broadcast_to(jnp.arange(N, dtype=jnp.int32)[:, None], (N, E))
        eid = jnp.broadcast_to(jnp.arange(E, dtype=jnp.int32)[None, :], (N, E))
        rank_c = jnp.where(keep, rank, cap)
        buf = jnp.full((E, cap), N, dtype=jnp.int32)
        buf = buf.at[eid, rank_c].set(tok, mode='drop')
        xpad = jnp.concatenate([xf, jnp.zeros((1, C), xf.dtype)], axis=0)
        xg = xpad[buf]
        h = jax.nn.gelu(jnp.einsum('ecd,edh->ech', xg, W1) + b1[:, None, :], approximate=False)
        out = jnp.einsum('ech,ehd->ecd', h, W2) + b2[:, None, :]
        rw_pad = jnp.concatenate([rw, jnp.zeros((1, E), rw.dtype)], axis=0)
        w = rw_pad[buf, jnp.arange(E, dtype=jnp.int32)[:, None]]
        weighted = out * w[..., None]
        final = jnp.zeros((N + 1, C), xf.dtype).at[buf.reshape(-1)].add(weighted.reshape(-1, C))
        return final[:N].reshape(B, T, C)
    h = _L0_tok_ref(x, L0_tok_W, L0_tok_b, L0_tok_cls_token, L0_tok_pos_embed)
    h = jnp.concatenate([jnp.broadcast_to(cls_tok, (h.shape[0], 1, h.shape[2])), h], axis=1)
    h = h + _L0_attn_ref(_layernorm(h, axis=-1), L0_attn_w_q, L0_attn_w_k, L0_attn_w_v, L0_attn_w_o)
    h = h + _L0_ffn_ref(_layernorm(h, axis=-1), L0_ffn_Wr, L0_ffn_br, L0_ffn_W1, L0_ffn_b1, L0_ffn_W2, L0_ffn_b2)
    return h

_drawn_inputs = setup_inputs


def setup_inputs(seed=0):
    import zlib

    import numpy as np

    out = dict(_drawn_inputs(seed))
    spreads = {'L0_ffn_br': (0.0, 0.1), 'L0_ffn_b1': (0.0, 0.714), 'L0_ffn_b2': (0.0, 0.267)}
    factors = {'L0_tok_b': 4.497}
    for name, (base, spread) in spreads.items():
        noise = np.random.default_rng([zlib.crc32(name.encode()), seed]).standard_normal(out[name].shape)
        drawn = base * np.exp(spread * noise) if base else spread * noise
        out[name] = jnp.asarray(drawn.astype(out[name].dtype))
    for name, factor in factors.items():
        out[name] = (out[name] * factor).astype(out[name].dtype)
    return out
```

```python
from contextlib import ExitStack

import concourse.bass as bass
from concourse import mybir

ALU = mybir.AluOpType
ACT = mybir.ActivationFunctionType
AX = mybir.AxisListType
F32 = mybir.dt.float32
BF16 = mybir.dt.bfloat16
I32 = mybir.dt.int32
U32 = mybir.dt.uint32

P = 128
EPS = 1e-5
MASKED = -1e30


def vit_block(nc, x, cls_tok, tok_w, tok_b, tok_cls, pos, wq, wk, wv, wo, wr, br, w1, b1, w2, b2, out):
    B, C, IMG, _ = x.shape
    D, PD = tok_w.shape
    S = pos.shape[1] + 1
    SIDE = int(round((PD // C) ** 0.5))
    NPH = IMG // SIDE
    H, _, DK = wq.shape
    E, _, HID = w1.shape
    N = B * S
    CAP = N * 2 // E
    HALF = CAP // 2
    KD = D // P
    KC = PD // P
    MH = HID // P
    PAIRS = H * DK // P
    TILES = -(-N // P)
    rows_of = [min(P, N - P * t) for t in range(TILES)]
    GB = P // S
    GT = GB * S
    GROUPS = -(-B // GB)
    tokens_of = [min(GT, N - GT * g) for g in range(GROUPS)]
    UNITS = 2 * GROUPS
    HU = H // 2
    HB = HU // 2
    NH = N // 2
    REC = D + 2
    TRASH = E * CAP
    assert KC == 2 * C and 2 * HALF == CAP and D == 2 * P and NPH * NPH + 2 == S and B * NPH <= P

    table = nc.dram_tensor("slot_table", [TRASH + 2 * N, REC], F32, kind="Internal").ap()

    with ExitStack() as ctx:
        def sb(name, shape, dt=F32):
            return ctx.enter_context(nc.sbuf_tensor(name, shape, dt))

        def sem(name):
            return ctx.enter_context(nc.semaphore(name))

        bank = [ctx.enter_context(nc.psum_tensor(f"bank{i}", [P, 512], F32)) for i in range(8)]

        xcols, imcols = KC * N, C * SIDE * IMG
        early = sb("early", [P, max(2 * PAIRS * N, imcols + xcols + KD * PD + KC * D)])
        images = early[0:B * NPH, 0:imcols].rearrange("p (c i w) -> p c i w", c=C, i=SIDE)
        patchT = early[:, imcols:imcols + xcols].rearrange("p (k n) -> p k n", k=KC)
        at = imcols + xcols
        w_in = early[:, at:at + KD * PD].rearrange("p (k n) -> p k n", k=KD)
        at += KD * PD
        w_inT = early[:, at:at + KC * D].rearrange("p (k n) -> p k n", k=KC)
        qT = early[:, 0:PAIRS * N].rearrange("p (h n) -> p h n", h=PAIRS)
        kT = early[:, PAIRS * N:2 * PAIRS * N].rearrange("p (h n) -> p h n", h=PAIRS)
        at = 2 * MH * CAP
        hidT = early[:, 0:at].rearrange("p (b m n) -> p b m n", b=2, m=MH)
        slotT = early[:, at:at + 2 * KD * CAP].rearrange("p (b k n) -> p b k n", b=2, k=KD)
        at += 2 * KD * CAP
        outT = early[:, at:at + 2 * KD * CAP].rearrange("p (b k n) -> p b k n", b=2, k=KD)
        at += 2 * KD * CAP
        y_sb = early[0:HALF, at:at + 4 * D].rearrange("p (b s d) -> p b s d", b=2, s=2)

        wq_sb = sb("wq_sb", [P, KD, H, DK])
        wk_sb = sb("wk_sb", [P, KD, H, DK])
        wv_sb = sb("wv_sb", [P, KD, H, DK])
        wo_sb = sb("wo_sb", [P, PAIRS, D])
        wr_sb = sb("wr_sb", [P, KD, E])
        br_sb = sb("br_sb", [P, E])
        h_sb = sb("h_sb", [P, TILES, D])
        xn_sb = sb("xn_sb", [P, TILES, D])
        xnT = sb("xnT", [P, KD, N])
        v_sb = sb("v_sb", [P, 3, HU * DK])
        prob = sb("prob", [P, 2, 2, HB * GT])
        probT = sb("probT", [P, 2, 2, HB * GT])
        zT = sb("zT", [P, PAIRS, N])
        rec = sb("rec", [P, TILES, 2, REC])
        patches = zT[0:B * NPH, :, :].rearrange("p k n -> p (k n)")[:, 0:imcols].rearrange("p (c w n) -> p c w n", c=C, w=NPH)
        xn2T = sb("xn2T", [P, KD * P])
        w1_sb = sb("w1_sb", [P, 2, KD, HID])
        w2_sb = sb("w2_sb", [P, 2, MH, D])
        bias_rows = sb("bias_rows", [P, P])
        biasT = sb("biasT", [P, E * (MH + KD)])
        slots = sb("slots", [HALF, 2, 2, REC])
        slot_meta = sb("slot_meta", [HALF, E, 2, 2])
        token = sb("token", [HALF, 2, 2], U32)
        ident = sb("ident", [P, P])
        spread = sb("spread", [S, B, S])
        base = sb("base", [S, D])
        base_add = sb("base_add", [S, D])
        own = sb("own", [P, GT], BF16)
        other = sb("other", [P, HB * GT], BF16)
        before = sb("before", [P, P], BF16)
        ones = sb("ones", [P, P], BF16)
        eps = sb("eps", [P, 1])
        expert_no = sb("expert_no", [P, E])
        slot_base = sb("slot_base", [P, TILES, E])
        trash_row = sb("trash_row", [P, TILES])
        blank = sb("blank", [HALF, 2, REC])
        stats = sb("stats", [P, 6])
        mv = sb("mv", [P, 2 * TILES, 2])
        lnv = sb("lnv", [P, 2 * TILES])
        rstd0 = sb("rstd0", [P, 2 * TILES])
        newton = sb("newton", [P, 2])
        rstd = sb("rstd", [P, 2 * TILES])
        negmax = sb("negmax", [P, UNITS, HU])
        den = sb("den", [P, UNITS, HU])
        rden = sb("rden", [P, UNITS, HU])
        logits = sb("logits", [P, E])
        top = sb("top", [P, 8])
        topi = sb("topi", [P, 8], U32)
        topf = sb("topf", [P, 2])
        first = sb("first", [P, TILES, E])
        second = sb("second", [P, TILES, E])
        chosen = sb("chosen", [P, TILES, E], BF16)
        chosen_sum = sb("chosen_sum", [P, TILES, E], BF16)
        gap = sb("gap", [P, TILES])
        egap = sb("egap", [P, TILES])
        gsum = sb("gsum", [P, 1])
        where = sb("where", [P, E])
        kept = sb("kept", [P, E])
        picked = sb("picked", [P, E])
        row = sb("row", [P, 2])
        trash_more = sb("trash_more", [P, 2])
        more = sb("more", [P, 2])
        row_no = sb("row_no", [P, TILES, 2], U32)

        x_in = [sem(f"x_in{c}") for c in range(C)]
        w_in_in, wq_in, wk_in, wv_in, wo_in = (sem(n) for n in ("w_in_in", "wq_in", "wk_in", "wv_in", "wo_in"))
        small_in = sem("small_in")
        base_in = sem("base_in")
        w1_in = [sem(f"w1_in{i}") for i in range(2)]
        w2_in = [sem(f"w2_in{i}") for i in range(2)]
        meta_in = sem("meta_in")
        slots_in = [sem(f"slots_in{i}") for i in range(2)]
        zeroed, ident_made, patch_zeroed, const_made = (sem(n) for n in ("zeroed", "ident_made", "patch_zeroed", "const_made"))
        zeroed_dve = sem("zeroed_dve")
        base_made = sem("base_made")
        sorted_act, sorted_dve = sem("sorted_act"), sem("sorted_dve")
        filled = sem("filled")
        evac_dve, evac_act = sem("evac_dve"), sem("evac_act")
        dve_chain = sem("dve_chain")
        pool_chain = sem("pool_chain")
        act_chain = sem("act_chain")
        var_made, rstd_made = sem("var_made"), sem("rstd_made")
        xn_made, hx_made = sem("xn_made"), sem("hx_made")
        scored, maxed, exped, rden_made, prob_made = (sem(n) for n in ("scored", "maxed", "exped", "rden_made", "prob_made"))
        flipped, probT_made, z_done, z_made = (sem(n) for n in ("flipped", "probT_made", "z_done", "z_made"))
        g_filled, g_evac = sem("g_filled"), sem("g_evac")
        rec_made, rec_copied, gap_made, egap_made, chosen_made, gates_made = (
            sem(n) for n in ("rec_made", "rec_copied", "gap_made", "egap_made", "chosen_made", "gates_made"))
        rows_made = sem("rows_made")
        blanked = sem("blanked")
        scattered = sem("scattered")
        h2_out = sem("h2_out")
        slotT_filled, slotT_made = sem("slotT_filled"), sem("slotT_made")
        hid_filled, hid_made, out_filled, outT_made = (sem(n) for n in ("hid_filled", "hid_made", "out_filled", "outT_made"))
        y_filled, y_made, added = sem("y_filled"), sem("y_made"), sem("added")

        uses = []
        for c in range(C):
            uses.append(("w", c, "dve"))
            for k in (2 * c, 2 * c + 1):
                uses += [("x", (k, 0), "act"), ("x", (k, 1), "dve")]
        uses += [("bias", 0, "dve")]
        for t in range(TILES):
            uses += [("h", t, "act")]
        for t in range(TILES):
            uses += [("xn", t, "act")]
        for p in range(PAIRS):
            for half in range(2):
                uses += [("q", (p, half), "act"), ("k", (p, half), "dve")]
        number = {(kind, what): i for i, (kind, what, _) in enumerate(uses)}

        def emptied(i):
            eng = uses[i][2]
            return (evac_dve if eng == "dve" else evac_act), sum(u[2] == eng for u in uses[:i + 1])

        g_uses = [("v", 0), ("v", 1)]
        for i in range(-1, UNITS):
            t = (i - 5) // 2
            if i >= 5 and i % 2 == 0:
                g_uses.append(("t", t))
            if i >= 7 and i % 2 == 1:
                g_uses.append(("r", t - 1))
            if 2 <= i + 2 < UNITS and i >= 0:
                g_uses.append(("v", i + 2))
            if i >= 5:
                g_uses.append(("o", t) if i % 2 else ("l", t))
        last = TILES - 1
        g_uses += [("t", last - 1), ("l", last - 1), ("r", last - 1), ("o", last), ("t", last), ("l", last), ("r", last)]
        g_number = {u: i for i, u in enumerate(g_uses)}
        assert len(g_number) == len(g_uses)
        G = bank[7]
        Z = bank[6]

        def span(i):
            return GT * (i // 2), tokens_of[i // 2], i % 2

        def patch_cols(dst, k, part):
            v = dst[:, k, :].rearrange("p (b s) -> p b s", s=S)[:, :, 2:S]
            return v.rearrange("p b (f w) -> p w b f", w=NPH)[:, 3 * part:3 * part + 3]

        def pixels(c, part):
            src = images[:, c].rearrange("p i (w j) -> p w i j", j=SIDE)[:, 3 * part:3 * part + 3]
            return patches[:, c, 3 * part:3 * part + 3, :].rearrange("p w (i j) -> p w i j", i=SIDE), src

        block = ctx.enter_context(nc.Block())

        @block.sync
        def _(sp):
            for c in range(C):
                sp.dma_start(images[:, c], x[:, c].rearrange("b (f i) w -> b f (i w)", i=SIDE)).then_inc(x_in[c], 16)
            for w, dst, done in ((wq, wq_sb, wq_in), (wk, wk_sb, wk_in), (wv, wv_sb, wv_in)):
                sp.dma_start(dst[:, 0], w[:, 0:P, :].rearrange("h p k -> p h k")).then_inc(done, 16)
                sp.dma_start(dst[:, 1], w[:, P:D, :].rearrange("h p k -> p h k")).then_inc(done, 16)
            sp.dma_start(wo_sb[:, :, :], wo.rearrange("(t p) d -> p t d", p=P)).then_inc(wo_in, 16)
            for e in range(2):
                sp.dma_start(w1_sb[:, e], w1[e].rearrange("(k p) n -> p k n", p=P)).then_inc(w1_in[e], 16)
                sp.dma_start(w2_sb[:, e], w2[e].rearrange("(m p) n -> p m n", p=P)).then_inc(w2_in[e], 16)
            sp.wait_ge(const_made, 1)
            for s in range(2):
                sp.dma_start(table[0:TRASH, :].rearrange("(e s p) c -> s p e c", p=HALF, s=2)[s],
                             blank[:, s:s + 1, :].to_broadcast([HALF, E, REC])).then_inc(blanked, 16)
            sp.dma_start(out[N:N + CAP, :].rearrange("(s p) d -> p s d", p=HALF), blank[:, :, 0:D]).then_inc(h2_out, 16)
            for t in range(TILES):
                sp.wait_ge(g_evac, g_number["o", t] + 1)
                sp.dma_start(out[P * t:P * t + rows_of[t], :], h_sb[0:rows_of[t], t, :]).then_inc(h2_out, 16)

            def load_slots(e, b):
                src = table[bass.ds(e * CAP, CAP), :].rearrange("(s p) c -> p s c", p=HALF)
                sp.dma_start(slots[:, b], src).then_inc(slots_in[b], 16)

            sp.wait_ge(scattered, 16 * 2 * TILES)
            load_slots(0, 0)
            sp.dma_start(slot_meta[:, :, :, :], table[0:TRASH, D:REC].rearrange("(e s p) c -> p e s c", p=HALF, s=2)).then_inc(meta_in, 16)
            load_slots(1, 1)

            def refill(e, b):
                sp.wait_ge(slotT_filled, e + 1)
                load_slots(e + 2, b)
                sp.wait_ge(hid_filled, MH // 2 * (e + 1))
                sp.dma_start(w1_sb[:, b], w1[bass.ds(e + 2, 1)].rearrange("a (k p) n -> p (a k) n", p=P)).then_inc(w1_in[b], 16)
                sp.wait_ge(out_filled, e + 1)
                sp.dma_start(w2_sb[:, b], w2[bass.ds(e + 2, 1)].rearrange("a (m p) n -> p (a m) n", p=P)).then_inc(w2_in[b], 16)

            with sp.Fori(0, E - 3, 2) as e:
                refill(e, 0)
                refill(e + 1, 1)
            sp.wait_ge(h2_out, 16 * (TILES + 1))
            sp.wait_ge(added, 32 * E)

        @block.gpsimd
        def _(pool):
            count = [0]

            def chained(ins):
                count[0] += 1
                ins.then_inc(pool_chain, 1)
                pool.wait_ge(pool_chain, count[0])

            nc.gpsimd.memset(ident[:, :], 0.0).then_inc(zeroed, 1)
            pool.wait_ge(zeroed, 1)
            nc.gpsimd.affine_select(out=ident[:, :], in_=ident[:, :], compare_op=ALU.not_equal, fill=1.0, base=0,
                                    pattern=[[1, P]], channel_multiplier=-1).then_inc(ident_made, 1)
            nc.gpsimd.memset(patchT[:, :, :].rearrange("p k (b s) -> p (k b) s", s=S)[:, :, 0:2], 0.0).then_inc(patch_zeroed, 1)
            chained(nc.gpsimd.memset(spread[:, :, :], 0.0))
            chained(nc.gpsimd.affine_select(out=spread[:, :, :], in_=spread[:, :, :], compare_op=ALU.not_equal, fill=1.0,
                                            base=0, pattern=[[0, B], [1, S]], channel_multiplier=-1))
            nc.gpsimd.memset(eps[:, :], EPS)
            for lo in (0, P // 2):
                o3 = own[lo:lo + GB, :].rearrange("p (a s) -> p a s", s=S)
                m3 = other[lo:lo + GB, :].rearrange("p (h a s) -> p h a s", a=GB, s=S)
                chained(nc.gpsimd.memset(o3, 0.0))
                chained(nc.gpsimd.affine_select(out=o3, in_=o3, compare_op=ALU.not_equal, fill=1.0, base=0,
                                                pattern=[[1, GB], [0, S]], channel_multiplier=-1))
                chained(nc.gpsimd.memset(m3, MASKED))
                chained(nc.gpsimd.affine_select(out=m3, in_=m3, compare_op=ALU.not_equal, fill=0.0, base=0,
                                                pattern=[[0, HB], [1, GB], [0, S]], channel_multiplier=-1))
            chained(nc.gpsimd.memset(ones[:, :], 1.0))
            chained(nc.gpsimd.affine_select(out=before[:, :], in_=ones[:, :], compare_op=ALU.is_ge, fill=0.0, base=-1,
                                            pattern=[[1, P]], channel_multiplier=-1))
            nc.gpsimd.iota(expert_no[:, :], pattern=[[1, E]], base=0, channel_multiplier=0,
                           allow_small_or_imprecise_dtypes=True)
            nc.gpsimd.iota(slot_base[:, :, :], pattern=[[-P, TILES], [CAP, E]], base=-TRASH, channel_multiplier=-1,
                           allow_small_or_imprecise_dtypes=True)
            nc.gpsimd.iota(trash_row[:, :], pattern=[[P, TILES]], base=TRASH, channel_multiplier=1,
                           allow_small_or_imprecise_dtypes=True)
            nc.gpsimd.iota(trash_more[:, :], pattern=[[N, 2]], base=0, channel_multiplier=0,
                           allow_small_or_imprecise_dtypes=True)
            nc.gpsimd.iota(rec[:, :, :, D].bitcast(I32), pattern=[[P, TILES], [0, 2]], base=0, channel_multiplier=1)
            chained(nc.gpsimd.memset(blank[:, :, :], 0.0))
            chained(nc.gpsimd.iota(blank[:, :, D].bitcast(I32), pattern=[[HALF, 2]], base=N, channel_multiplier=1))
            nc.gpsimd.memset(chosen_sum[:, 0, :], 0.0).then_inc(const_made, 1)

            def residual(t):
                r = rows_of[t]
                pool.wait_ge(xn_made, t + 1)
                nc.gpsimd.tensor_tensor(h_sb[0:r, t, :], h_sb[0:r, t, :], xn_sb[0:r, t, :], ALU.add).then_inc(hx_made, 1)

            for t in range(TILES):
                residual(t)

            def normalise(i):
                _, T, b = span(i)
                for par in range(2):
                    pool.wait_ge(rden_made, 2 * i + par + 1)
                    v = prob[0:T, b, par, 0:HB * T].rearrange("p (h m) -> p h m", h=HB)
                    r = rden[0:T, i, HB * par:HB * par + HB].rearrange("p (h a) -> p h a", a=1).to_broadcast([T, HB, T])
                    nc.gpsimd.tensor_tensor(v, v, r, ALU.mult).then_inc(prob_made, 1)

            def second_record(t):
                r = rows_of[t]
                pool.wait_ge(rec_made, t + 1)
                nc.gpsimd.tensor_copy(rec[0:r, t, 1, 0:D], rec[0:r, t, 0, 0:D]).then_inc(rec_copied, 1)

            def scatter(t):
                r = rows_of[t]
                if t == 0:
                    pool.wait_ge(blanked, 32)
                pool.wait_ge(rec_copied, t + 1)
                pool.wait_ge(gates_made, t + 1)
                pool.wait_ge(rows_made, t + 1)
                for k in range(2):
                    pool.indirect_dma_start(
                        table, bass.IndirectOffsetOnAxis(ap=row_no[0:r, t, k:k + 1], axis=0),
                        rec[0:r, t, k, :], None).then_inc(scattered, 16)

            for i in range(UNITS):
                normalise(i)
                t = (i - 5) // 2
                if i >= 5 and i % 2 == 0:
                    second_record(t)
                if i >= 7 and i % 2 == 1:
                    scatter(t - 1)
            second_record(last - 1)
            scatter(last - 1)
            second_record(last)
            scatter(last)

            pool.wait_ge(h2_out, 16 * (TILES + 1))
            for e in range(E):
                pool.wait_ge(y_made, e + 1)
                if e:
                    pool.wait_ge(added, 32 * e)
                for s in range(2):
                    pool.indirect_dma_start(
                        out, bass.IndirectOffsetOnAxis(ap=token[:, e % 2, s:s + 1], axis=0),
                        y_sb[:, e % 2, s, :], None, compute_op=ALU.add).then_inc(added, 16)

        @block.scalar
        def _(act):
            act.dma_start(w_in[:, :, :], tok_w.rearrange("(k p) n -> p k n", p=P)).then_inc(w_in_in, 16)
            act.dma_start(base[1:S, :], pos[0]).then_inc(base_in, 16)
            act.dma_start(base[0:1, :], cls_tok[0]).then_inc(base_in, 16)
            act.dma_start(base_add[1:2, :], tok_cls[0]).then_inc(base_in, 16)
            act.dma_start(base_add[2:S, :], tok_b.rearrange("(a d) -> a d", a=1).to_broadcast([S - 2, D])).then_inc(base_in, 16)
            act.dma_start(bias_rows[0:E * MH, :], b1.rearrange("e (m p) -> (e m) p", p=P)).then_inc(small_in, 16)
            act.dma_start(bias_rows[E * MH:E * (MH + KD), :], b2.rearrange("e (m p) -> (e m) p", p=P)).then_inc(small_in, 16)
            act.dma_start(wr_sb[:, :, :], wr.rearrange("(k p) e -> p k e", p=P)).then_inc(small_in, 16)
            act.dma_start(br_sb[:, :], br.rearrange("(a e) -> a e", a=1).to_broadcast([P, E])).then_inc(small_in, 16)

            count = [0]

            def chained(ins):
                count[0] += 1
                ins.then_inc(act_chain, 1)
                act.wait_ge(act_chain, count[0])

            def patches_out(k, part):
                i = number["x", (k, part)]
                act.wait_ge(filled, i + 1)
                src = bank[i % 8][:, 0:3 * B * NPH].rearrange("p (w b f) -> p w b f", w=3, b=B)
                nc.scalar.copy(patch_cols(patchT, k, part), src).then_inc(evac_act, 1)

            def sort(c):
                act.wait_ge(x_in[c], 16)
                nc.scalar.copy(*pixels(c, 0)).then_inc(sorted_act, 1)

            sort(0)
            sort(1)
            act.wait_ge(patch_zeroed, 1)
            for c in range(C):
                patches_out(2 * c, 0)
                patches_out(2 * c + 1, 0)
                if c + 2 < C:
                    sort(c + 2)

            def rstd_guess(j, r):
                act.wait_ge(var_made, j + 1)
                chained(nc.scalar.activation(lnv[0:r, j:j + 1], mv[0:r, j, 1:2], ACT.Ln, bias=eps[0:r, :]))
                nc.scalar.activation(rstd0[0:r, j:j + 1], lnv[0:r, j:j + 1], ACT.Exp, scale=-0.5).then_inc(rstd_made, 1)

            def h_out(t):
                i = number["h", t]
                r = rows_of[t]
                act.wait_ge(filled, i + 1)
                nc.scalar.copy(h_sb[0:r, t, :], bank[i % 8][0:r, 0:D]).then_inc(evac_act, 1)

            act.wait_ge(const_made, 1)
            for t in range(TILES):
                h_out(t)
                rstd_guess(t, rows_of[t])
            for t in range(TILES):
                i, r = number["xn", t], rows_of[t]
                act.wait_ge(filled, i + 1)
                nc.scalar.copy(xnT[:, :, P * t:P * t + r], bank[i % 8][:, 0:KD * r].rearrange("p (k n) -> p k n", k=KD)).then_inc(evac_act, 1)
            for p in range(PAIRS):
                for half in range(2):
                    i = number["q", (p, half)]
                    act.wait_ge(filled, i + 1)
                    nc.scalar.mul(qT[:, p, NH * half:NH * half + NH], bank[i % 8][:, 0:NH], float(DK) ** -0.5).then_inc(evac_act, 1)

            def exponentials(i):
                _, T, b = span(i)
                for par in range(2):
                    act.wait_ge(maxed, 2 * i + par + 1)
                    if i >= 2:
                        act.wait_ge(flipped, 2 * (i - 2) + par + 1)
                    for h in range(HB):
                        j = HB * par + h
                        ins = nc.scalar.activation(prob[0:T, b, par, h * T:h * T + T], bank[2 * b + par][0:T, h * T:h * T + T],
                                                   ACT.Exp, bias=negmax[0:T, i, j:j + 1], accum_out=den[0:T, i, j:j + 1])
                    ins.then_inc(exped, 1)

            def z_out(i):
                o, T, _ = span(i)
                act.wait_ge(z_done, i + 1)
                nc.scalar.copy(zT[:, HB * (i % 2):HB * (i % 2) + HB, o:o + T],
                               Z[:, 0:HB * T].rearrange("p (h n) -> p h n", h=HB)).then_inc(z_made, 1)

            def gate_exp(t):
                r = rows_of[t]
                act.wait_ge(gap_made, t + 1)
                nc.scalar.activation(egap[0:r, t:t + 1], gap[0:r, t:t + 1], ACT.Exp).then_inc(egap_made, 1)

            for i in range(-1, UNITS):
                t = (i - 5) // 2
                if i + 1 < UNITS:
                    exponentials(i + 1)
                if i >= 7 and i % 2 == 1:
                    gate_exp(t - 1)
                if i >= 1:
                    z_out(i - 1)
                if i >= 5 and i % 2 == 1:
                    rstd_guess(TILES + t, rows_of[t])
            gate_exp(last - 1)
            z_out(UNITS - 1)
            rstd_guess(TILES + last, rows_of[last])
            gate_exp(last)

            def gelu(e, b):
                for j in range(MH // 2):
                    act.wait_ge(hid_filled, MH // 2 * e + j + 1)
                    for m in (2 * j, 2 * j + 1):
                        bias = biasT[:, bass.ds(e * MH + m, 1)]
                        ins = nc.scalar.activation(hidT[:, b, m, :], bank[j][:, (m % 2) * CAP:(m % 2) * CAP + CAP], ACT.Gelu, bias=bias)
                    ins.then_inc(hid_made, 1)

            gelu(0, 0)
            gelu(1, 1)
            with act.Fori(2, E - 1, 2) as e:
                act.wait_ge(out_filled, e - 1)
                gelu(e, 0)
                act.wait_ge(out_filled, e)
                gelu(e + 1, 1)

        @block.vector
        def _(dve):
            count = [0]

            def chained(ins):
                count[0] += 1
                ins.then_inc(dve_chain, 1)
                dve.wait_ge(dve_chain, count[0])

            chained(nc.vector.memset(base_add[0:1, :], 0.0))
            dve.wait_ge(base_in, 64)
            nc.vector.tensor_tensor(base[:, :], base[:, :], base_add[:, :], ALU.add).then_inc(base_made, 1)
            def sort(c):
                dve.wait_ge(x_in[c], 16)
                nc.vector.tensor_copy(*pixels(c, 1)).then_inc(sorted_dve, 1)

            sort(0)
            sort(1)
            dve.wait_ge(patch_zeroed, 1)
            for c in range(C):
                i = number["w", c]
                dve.wait_ge(filled, i + 1)
                nc.vector.tensor_copy(w_inT[:, 2 * c:2 * c + 2, :], bank[i % 8][:, 0:2 * D].rearrange("p (k n) -> p k n", k=2)).then_inc(evac_dve, 1)
                for k in (2 * c, 2 * c + 1):
                    i = number["x", (k, 1)]
                    dve.wait_ge(filled, i + 1)
                    src = bank[i % 8][:, 0:3 * B * NPH].rearrange("p (w b f) -> p w b f", w=3, b=B)
                    nc.vector.tensor_copy(patch_cols(patchT, k, 1), src).then_inc(evac_dve, 1)
                if c + 2 < C:
                    sort(c + 2)
            i = number["bias", 0]
            dve.wait_ge(filled, i + 1)
            nc.vector.tensor_copy(biasT[:, :], bank[i % 8][:, 0:E * (MH + KD)]).then_inc(evac_dve, 1)

            def variance(src, j, r):
                chained(nc.vector.bn_stats(stats[0:r, :], src))
                nc.vector.bn_aggr(mv[0:r, j, :], stats[0:r, :]).then_inc(var_made, 1)

            def layernorm(dst, src, j, r):
                dve.wait_ge(rstd_made, j + 1)
                chained(nc.vector.tensor_tensor(newton[0:r, 0:1], rstd0[0:r, j:j + 1], rstd0[0:r, j:j + 1], ALU.mult))
                chained(nc.vector.scalar_tensor_tensor(out=newton[0:r, 1:2], in0=mv[0:r, j, 1:2], scalar=EPS,
                                                       in1=newton[0:r, 0:1], op0=ALU.add, op1=ALU.mult))
                chained(nc.vector.tensor_scalar(newton[0:r, 0:1], newton[0:r, 1:2], -0.5, 1.5, ALU.mult, ALU.add))
                chained(nc.vector.tensor_tensor(rstd[0:r, j:j + 1], newton[0:r, 0:1], rstd0[0:r, j:j + 1], ALU.mult))
                return nc.vector.tensor_scalar(dst, src, mv[0:r, j, 0:1], rstd[0:r, j:j + 1], ALU.subtract, ALU.mult)

            for t in range(TILES):
                r = rows_of[t]
                sem_, value = emptied(number["h", t])
                dve.wait_ge(sem_, value)
                variance(h_sb[0:r, t, :], t, r)
                layernorm(xn_sb[0:r, t, :], h_sb[0:r, t, :], t, r).then_inc(xn_made, 1)
            for p in range(PAIRS):
                for half in range(2):
                    i = number["k", (p, half)]
                    dve.wait_ge(filled, i + 1)
                    nc.vector.tensor_copy(kT[:, p, NH * half:NH * half + NH], bank[i % 8][:, 0:NH]).then_inc(evac_dve, 1)

            def row_max(i):
                _, T, b = span(i)
                for par in range(2):
                    dve.wait_ge(scored, 2 * i + par + 1)
                    nc.vector.tensor_reduce(negmax[0:T, i, HB * par:HB * par + HB],
                                            bank[2 * b + par][0:T, 0:HB * T].rearrange("p (h m) -> p h m", h=HB),
                                            AX.X, ALU.max, negate=True).then_inc(maxed, 1)

            def row_rden(i):
                _, T, _ = span(i)
                for par in range(2):
                    dve.wait_ge(exped, 2 * i + par + 1)
                    nc.vector.reciprocal(rden[0:T, i, HB * par:HB * par + HB], den[0:T, i, HB * par:HB * par + HB]).then_inc(rden_made, 1)

            def probT_out(i):
                _, T, b = span(i)
                for par in range(2):
                    dve.wait_ge(flipped, 2 * i + par + 1)
                    if i >= 2:
                        dve.wait_ge(z_done, i - 1)
                    nc.vector.tensor_copy(probT[0:T, b, par, 0:HB * T], bank[4 + par][0:T, 0:HB * T]).then_inc(probT_made, 1)

            def g_ready(what):
                dve.wait_ge(g_filled, g_number[what] + 1)

            def v_out(i):
                _, T, _ = span(i)
                g_ready(("v", i))
                if i >= 3:
                    dve.wait_ge(z_done, i - 2)
                nc.vector.tensor_copy(v_sb[0:T, i % 3, :], G[0:T, :]).then_inc(g_evac, 1)

            def h2_of(t):
                r = rows_of[t]
                g_ready(("o", t))
                dve.wait_ge(hx_made, t + 1)
                nc.vector.tensor_tensor(h_sb[0:r, t, :], h_sb[0:r, t, :], G[0:r, 0:D], ALU.add).then_inc(g_evac, 1)
                dve.wait_ge(g_evac, g_number["o", t] + 1)
                variance(h_sb[0:r, t, :], TILES + t, r)

            def second_layernorm(t):
                r = rows_of[t]
                layernorm(rec[0:r, t, 0, 0:D], h_sb[0:r, t, :], TILES + t, r).then_inc(rec_made, 1)

            def xn2T_out(t):
                r = rows_of[t]
                g_ready(("t", t))
                nc.vector.tensor_copy(xn2T[:, 0:KD * r], G[:, 0:KD * r]).then_inc(g_evac, 1)

            def choose(t):
                r = rows_of[t]
                g_ready(("l", t))
                nc.vector.tensor_tensor(logits[0:r, :], G[0:r, 0:E], br_sb[0:r, :], ALU.add).then_inc(g_evac, 1)
                dve.wait_ge(g_evac, g_number["l", t] + 1)
                chained(nc.vector.max(top[0:r, :], logits[0:r, :]))
                nc.vector.tensor_tensor(gap[0:r, t:t + 1], top[0:r, 1:2], top[0:r, 0:1], ALU.subtract).then_inc(gap_made, 1)
                chained(nc.vector.max_index(topi[0:r, :], top[0:r, :], logits[0:r, :]))
                chained(nc.vector.tensor_copy(topf[0:r, :], topi[0:r, 0:2]))
                nc.vector.tensor_scalar(second[0:r, t, :], expert_no[0:r, :], topf[0:r, 1:2], None, ALU.is_equal)
                chained(nc.vector.tensor_scalar(first[0:r, t, :], expert_no[0:r, :], topf[0:r, 0:1], None, ALU.is_equal))
                nc.vector.tensor_tensor(chosen[0:r, t, :], first[0:r, t, :], second[0:r, t, :], ALU.add).then_inc(chosen_made, 1)
                dve.wait_ge(chosen_made, t + 1)
                if t < last:
                    chained(nc.vector.tensor_tensor(chosen_sum[:, t + 1, :], chosen_sum[:, t, :], chosen[:, t, :], ALU.add))

            def gates(t):
                r = rows_of[t]
                dve.wait_ge(egap_made, t + 1)
                chained(nc.vector.tensor_scalar(gsum[0:r, :], egap[0:r, t:t + 1], 1.0, None, ALU.add))
                chained(nc.vector.reciprocal(rec[0:r, t, 0, D + 1:D + 2], gsum[0:r, :]))
                nc.vector.tensor_tensor(rec[0:r, t, 1, D + 1:D + 2], rec[0:r, t, 0, D + 1:D + 2], egap[0:r, t:t + 1],
                                        ALU.mult).then_inc(gates_made, 1)

            def slots_of(t):
                r = rows_of[t]
                g_ready(("r", t))
                chained(nc.vector.tensor_tensor(where[0:r, :], G[0:r, 0:E], slot_base[0:r, t, :], ALU.add))
                nc.vector.scalar_tensor_tensor(out=kept[0:r, :], in0=G[0:r, 0:E], scalar=float(CAP), in1=where[0:r, :],
                                               op0=ALU.is_lt, op1=ALU.mult).then_inc(g_evac, 1)
                dve.wait_ge(g_evac, g_number["r", t] + 1)
                for k, hot in enumerate((first, second)):
                    chained(nc.vector.tensor_tensor_reduce(picked[0:r, :], hot[0:r, t, :], kept[0:r, :], 1.0, 0.0,
                                                           ALU.mult, ALU.add, row[0:r, k:k + 1]))
                chained(nc.vector.scalar_tensor_tensor(out=more[0:r, :], in0=row[0:r, :], scalar=0.0, in1=trash_more[0:r, :],
                                                       op0=ALU.is_equal, op1=ALU.mult))
                nc.vector.scalar_tensor_tensor(out=row_no[0:r, t, :], in0=row[0:r, :], scalar=trash_row[0:r, t:t + 1],
                                               in1=more[0:r, :], op0=ALU.add, op1=ALU.add).then_inc(rows_made, 1)

            dve.wait_ge(small_in, 64)
            dve.wait_ge(const_made, 1)
            v_out(0)
            v_out(1)
            for i in range(-1, UNITS):
                t = (i - 5) // 2
                if i + 1 < UNITS:
                    row_max(i + 1)
                if i >= 5 and i % 2 == 0:
                    xn2T_out(t)
                if i >= 7 and i % 2 == 1:
                    slots_of(t - 1)
                if i >= 0:
                    row_rden(i)
                if i >= 0 and i + 2 < UNITS:
                    v_out(i + 2)
                if i >= 0:
                    probT_out(i)
                if i >= 7 and i % 2 == 1:
                    gates(t - 1)
                if i >= 5 and i % 2 == 1:
                    h2_of(t)
                    second_layernorm(t)
                if i >= 5 and i % 2 == 0:
                    choose(t)
            xn2T_out(last - 1)
            choose(last - 1)
            slots_of(last - 1)
            gates(last - 1)
            h2_of(last)
            second_layernorm(last)
            xn2T_out(last)
            choose(last)
            slots_of(last)
            gates(last)

            def slotT_out(e, b):
                dve.wait_ge(slotT_filled, e + 1)
                nc.vector.tensor_copy(slotT[:, b], bank[7][:, 0:KD * CAP].rearrange("p (k n) -> p k n", k=KD)).then_inc(slotT_made, 1)

            def outT_out(e, b):
                dve.wait_ge(out_filled, e + 1)
                for d in range(KD):
                    ins = nc.vector.tensor_scalar(outT[:, b, d, :], bank[4 + d][:, 0:CAP],
                                                  biasT[:, bass.ds(E * MH + e * KD + d, 1)], None, ALU.add)
                ins.then_inc(outT_made, 1)

            def y_out(e, b):
                dve.wait_ge(y_filled, e + 1)
                nc.vector.tensor_copy(token[:, b, :], slot_meta[:, bass.ds(e, 1), :, 0:1].rearrange("p a s c -> p (a s c)").bitcast(U32))
                for s in range(2):
                    ins = nc.vector.tensor_scalar(y_sb[:, b, s, :], bank[6][0:HALF, s * D:s * D + D],
                                                  slot_meta[:, bass.ds(e, 1), s, 1:2].rearrange("p a c -> p (a c)"), None, ALU.mult)
                ins.then_inc(y_made, 1)

            def mid(e, b):
                y_out(e - 1, 1 - b)
                slotT_out(e + 1, 1 - b)
                outT_out(e, b)

            slotT_out(0, 0)
            slotT_out(1, 1)
            dve.wait_ge(meta_in, 16)
            outT_out(0, 0)
            mid(1, 1)
            mid(2, 0)
            with dve.Fori(3, E - 2, 2) as e:
                dve.wait_ge(added, 32 * (e - 2))
                mid(e, 1)
                dve.wait_ge(added, 32 * (e - 1))
                mid(e + 1, 0)
            dve.wait_ge(added, 32 * (E - 3))
            y_out(E - 2, 0)
            outT_out(E - 1, 1)
            dve.wait_ge(added, 32 * (E - 2))
            y_out(E - 1, 1)

        @block.tensor
        def _(pe):
            def free(i):
                if i >= 8:
                    s, v = emptied(i - 8)
                    pe.wait_ge(s, v)

            pe.wait_ge(ident_made, 1)
            pe.wait_ge(w_in_in, 16)
            for c in range(C):
                i = number["w", c]
                free(i)
                for k in (2 * c, 2 * c + 1):
                    for m in range(KD):
                        o = (k % 2) * D + m * P
                        mm = pe.transpose(bank[i % 8][:, o:o + P], w_in[:, m, k * P:(k + 1) * P], ident[:, :])
                mm.then_inc(filled, 1)
                pe.wait_ge(sorted_act, c + 1)
                pe.wait_ge(sorted_dve, c + 1)
                for k in (2 * c, 2 * c + 1):
                    for part in range(2):
                        i = number["x", (k, part)]
                        free(i)
                        for w in range(3):
                            src = patches[:, c, 3 * part + w, P * (k % 2):P * (k % 2) + P]
                            mm = pe.transpose(bank[i % 8][:, w * B * NPH:(w + 1) * B * NPH], src, ident[0:B * NPH, 0:B * NPH])
                        mm.then_inc(filled, 1)
            i = number["bias", 0]
            free(i)
            pe.wait_ge(small_in, 64)
            pe.transpose(bank[i % 8][:, 0:E * (MH + KD)], bias_rows[0:E * (MH + KD), :],
                         ident[0:E * (MH + KD), 0:E * (MH + KD)]).then_inc(filled, 1)
            pe.wait_ge(base_made, 1)
            pe.wait_ge(const_made, 1)
            for s, v in (emptied(number["x", (KC - 1, 0)]), emptied(number["x", (KC - 1, 1)])):
                pe.wait_ge(s, v)
            spread_v = spread[:, :, :].rearrange("s b t -> s (b t)")
            for t in range(TILES):
                i, r = number["h", t], rows_of[t]
                free(i)
                for k in range(KC):
                    pe.matmul(bank[i % 8][0:r, 0:D], patchT[:, k, P * t:P * t + r], w_inT[:, k, :], start=(k == 0), stop=False)
                pe.matmul(bank[i % 8][0:r, 0:D], spread_v[:, P * t:P * t + r], base[:, :], start=False, stop=True).then_inc(filled, 1)
            for t in range(TILES):
                i, r = number["xn", t], rows_of[t]
                free(i)
                pe.wait_ge(xn_made, t + 1)
                for k in range(KD):
                    mm = pe.transpose(bank[i % 8][:, k * r:k * r + r], xn_sb[0:r, t, k * P:(k + 1) * P], ident[0:r, 0:r])
                mm.then_inc(filled, 1)
            s, v = emptied(number["xn", TILES - 1])
            pe.wait_ge(s, v)
            pe.wait_ge(wq_in, 32)
            pe.wait_ge(wk_in, 32)
            for p in range(PAIRS):
                for half in range(2):
                    for name, w in (("q", wq_sb), ("k", wk_sb)):
                        i = number[name, (p, half)]
                        free(i)
                        for k in range(KD):
                            mm = pe.matmul(bank[i % 8][:, 0:NH], w[:, k, 2 * p:2 * p + 2, :].rearrange("p h k -> p (h k)"),
                                           xnT[:, k, NH * half:NH * half + NH], start=(k == 0), stop=(k == KD - 1))
                        mm.then_inc(filled, 1)
            for name in ("q", "k"):
                s, v = emptied(number[name, (PAIRS - 1, 1)])
                pe.wait_ge(s, v)

            def g_free(what):
                if g_number[what]:
                    pe.wait_ge(g_evac, g_number[what])

            def values(i):
                o, T, _ = span(i)
                g_free(("v", i))
                for k in range(KD):
                    mm = pe.matmul(G[0:T, :], xnT[:, k, o:o + T],
                                   wv_sb[:, k, HU * (i % 2):HU * (i % 2) + HU, :].rearrange("p h k -> p (h k)"),
                                   start=(k == 0), stop=(k == KD - 1))
                mm.then_inc(g_filled, 1)

            def scores(i):
                o, T, b = span(i)
                if i >= 2:
                    pe.wait_ge(exped, 2 * (i - 1))
                masked = T > S
                if masked:
                    for par in range(2):
                        lo = par * (P // 2)
                        pe.matmul(bank[2 * b + par][0:T, 0:HB * T], own[lo:lo + GB, :], other[lo:lo + GB, :],
                                  start=True, stop=False)
                for h in range(HB):
                    for par in range(2):
                        lo, p = par * (P // 2), HB * (i % 2) + h
                        mm = pe.matmul(bank[2 * b + par][0:T, h * T:h * T + T], qT[lo:lo + DK, p, o:o + T], kT[lo:lo + DK, p, o:o + T],
                                       start=not masked, stop=(h == HB - 1 or not masked))
                        if h == HB - 1:
                            mm.then_inc(scored, 1)

            def flip(i):
                _, T, b = span(i)
                for par in range(2):
                    pe.wait_ge(prob_made, 2 * i + par + 1)
                    if i >= 1:
                        pe.wait_ge(probT_made, 2 * (i - 1) + par + 1)
                    for h in range(HB):
                        mm = pe.transpose(bank[4 + par][0:T, h * T:h * T + T], prob[0:T, b, par, h * T:h * T + T], ident[0:T, 0:T])
                    mm.then_inc(flipped, 1)

            def weigh(i):
                _, T, b = span(i)
                pe.wait_ge(probT_made, 2 * i + 2)
                pe.wait_ge(g_evac, g_number["v", i] + 1)
                if i >= 1:
                    pe.wait_ge(z_made, i)
                for h in range(HB):
                    for par in range(2):
                        lo, c = par * (P // 2), (2 * h + par) * DK
                        mm = pe.matmul(Z[lo:lo + DK, h * T:h * T + T], v_sb[0:T, i % 3, c:c + DK], probT[0:T, b, par, h * T:h * T + T],
                                       start=True, stop=True)
                mm.then_inc(z_done, 1)

            def attention_out(t):
                r = rows_of[t]
                g_free(("o", t))
                pe.wait_ge(z_made, min(2 * (t + 2), UNITS))
                for p in range(PAIRS):
                    mm = pe.matmul(G[0:r, 0:D], zT[:, p, P * t:P * t + r], wo_sb[:, p, :], start=(p == 0), stop=(p == PAIRS - 1))
                mm.then_inc(g_filled, 1)

            def flip_xn2(t):
                r = rows_of[t]
                g_free(("t", t))
                pe.wait_ge(rec_made, t + 1)
                for k in range(KD):
                    mm = pe.transpose(G[:, k * r:k * r + r], rec[0:r, t, 0, k * P:(k + 1) * P], ident[0:r, 0:r])
                mm.then_inc(g_filled, 1)

            def router(t):
                r = rows_of[t]
                g_free(("l", t))
                for k in range(KD):
                    mm = pe.matmul(G[0:r, 0:E], xn2T[:, k * r:k * r + r], wr_sb[:, k, :], start=(k == 0), stop=(k == KD - 1))
                mm.then_inc(g_filled, 1)

            def ranks(t):
                r = rows_of[t]
                g_free(("r", t))
                pe.wait_ge(chosen_made, t + 1)
                pe.matmul(G[0:r, 0:E], before[0:r, 0:r], chosen[0:r, t, :], start=True, stop=False)
                pe.matmul(G[0:r, 0:E], ones[:, 0:r], chosen_sum[:, t, :], start=False, stop=True).then_inc(g_filled, 1)

            pe.wait_ge(wv_in, 32)
            pe.wait_ge(wo_in, 16)
            values(0)
            values(1)
            for i in range(-1, UNITS):
                t = (i - 5) // 2
                if i + 1 < UNITS:
                    scores(i + 1)
                if i >= 5 and i % 2 == 0:
                    flip_xn2(t)
                if i >= 7 and i % 2 == 1:
                    ranks(t - 1)
                if i >= 1:
                    weigh(i - 1)
                if i >= 0 and i + 2 < UNITS:
                    values(i + 2)
                if i >= 0:
                    flip(i)
                if i >= 5 and i % 2 == 1:
                    attention_out(t)
                if i >= 5 and i % 2 == 0:
                    router(t)
            flip_xn2(last - 1)
            router(last - 1)
            ranks(last - 1)
            weigh(UNITS - 1)
            attention_out(last)
            flip_xn2(last)
            router(last)
            ranks(last)

            def flip_slots(e, b, n):
                pe.wait_ge(slots_in[b], 16 * n)
                for k in range(KD):
                    for s in range(2):
                        o = k * CAP + s * HALF
                        mm = pe.transpose(bank[7][:, o:o + HALF], slots[:, b, s, k * P:(k + 1) * P], ident[0:HALF, 0:HALF])
                mm.then_inc(slotT_filled, 1)

            def up(e, b, n, first_one=False):
                pe.wait_ge(w1_in[b], 16 * n)
                pe.wait_ge(slotT_made, e + 1)
                for m in range(MH):
                    j = m // 2
                    if m % 2 == 0 and not first_one:
                        pe.wait_ge(hid_made, MH // 2 * (e - 1) + j + 1)
                    for k in range(KD):
                        mm = pe.matmul(bank[j][:, (m % 2) * CAP:(m % 2) * CAP + CAP], w1_sb[:, b, k, m * P:(m + 1) * P], slotT[:, b, k, :],
                                       start=(k == 0), stop=(k == KD - 1))
                    if m % 2:
                        mm.then_inc(hid_filled, 1)

            def down(e, b, n, first_one=False):
                pe.wait_ge(w2_in[b], 16 * n)
                if not first_one:
                    pe.wait_ge(outT_made, e)
                for m in range(MH):
                    if m % 2 == 0:
                        pe.wait_ge(hid_made, MH // 2 * e + m // 2 + 1)
                    for d in range(KD):
                        mm = pe.matmul(bank[4 + d][:, 0:CAP], w2_sb[:, b, m, d * P:(d + 1) * P], hidT[:, b, m, :],
                                       start=(m == 0), stop=(m == MH - 1))
                mm.then_inc(out_filled, 1)

            def flip_out(e, b):
                pe.wait_ge(outT_made, e + 1)
                for s in range(2):
                    for d in range(KD):
                        o = s * D + d * P
                        mm = pe.transpose(bank[6][0:HALF, o:o + P], outT[:, b, d, s * HALF:(s + 1) * HALF], ident[:, :])
                mm.then_inc(y_filled, 1)

            def expert(e, b, n, n_next):
                up(e, b, n)
                pe.wait_ge(y_made, e - 1) if not isinstance(e, int) or e > 1 else None
                flip_out(e - 1, 1 - b)
                flip_slots(e + 1, 1 - b, n_next)
                down(e, b, n)

            pe.wait_ge(g_evac, len(g_uses))
            flip_slots(0, 0, 1)
            up(0, 0, 1, first_one=True)
            pe.wait_ge(slotT_made, 1)
            flip_slots(1, 1, 1)
            down(0, 0, 1, first_one=True)
            expert(1, 1, 1, 2)
            with pe.Fori(2, E - 3, 2) as e:
                expert(e, 0, (e >> 1) + 1, (e >> 1) + 1)
                expert(e + 1, 1, (e >> 1) + 1, (e >> 1) + 2)
            expert(E - 2, 0, E // 2, E // 2)
            up(E - 1, 1, E // 2)
            pe.wait_ge(y_made, E - 2)
            flip_out(E - 2, 0)
            down(E - 1, 1, E // 2)
            pe.wait_ge(y_made, E - 1)
            flip_out(E - 1, 1)


_INS = ["x", "cls_tok", "L0_tok_W", "L0_tok_b", "L0_tok_cls_token", "L0_tok_pos_embed", "L0_attn_w_q", "L0_attn_w_k",
        "L0_attn_w_v", "L0_attn_w_o", "L0_ffn_Wr", "L0_ffn_br", "L0_ffn_W1", "L0_ffn_b1", "L0_ffn_W2", "L0_ffn_b2"]


def kernel(**inputs):
    import numpy as _np
    import concourse.bacc as _bacc
    from concourse import mybir as _mybir
    from concourse.bass_utils import run_bass_kernel_spmd as _run

    nc = _bacc.Bacc("TRN2", target_bir_lowering=False, num_devices=1)
    arrays, args = {}, []
    for name in _INS:
        a = _np.ascontiguousarray(inputs[name])
        arrays[f"in_{name}_dram"] = a
        args.append(nc.dram_tensor(f"in_{name}_dram", a.shape, _mybir.dt.from_np(a.dtype), kind="ExternalInput").ap())
    images = inputs["x"].shape[0]
    tokens = inputs["L0_tok_pos_embed"].shape[1] + 1
    experts = inputs["L0_ffn_W1"].shape[0]
    dim = inputs["cls_tok"].shape[2]
    n = images * tokens
    out = nc.dram_tensor("out_0_dram", (n + n * 2 // experts, dim), _mybir.dt.float32, kind="ExternalOutput").ap()
    vit_block(nc, *args, out)
    r = _run(nc, [arrays], core_ids=[0])
    return r.results[0]["out_0_dram"][:n].reshape(images, tokens, dim)
```

```python
from contextlib import ExitStack

import concourse.bass as bass
from concourse import mybir

ALU = mybir.AluOpType
ACT = mybir.ActivationFunctionType
AX = mybir.AxisListType
F32 = mybir.dt.float32
F32R = mybir.dt.float32r
BF16 = mybir.dt.bfloat16
I32 = mybir.dt.int32
U32 = mybir.dt.uint32

P = 128
EPS = 1e-5
MASKED = -1e30


def vit_block(nc, x, cls_tok, tok_w, tok_b, tok_cls, pos, wq, wk, wv, wo, wr, br, w1, b1, w2, b2, out):
    B, C, IMG, _ = x.shape
    D, PD = tok_w.shape
    S = pos.shape[1] + 1
    SIDE = int(round((PD // C) ** 0.5))
    NPH = IMG // SIDE
    H, _, DK = wq.shape
    E, _, HID = w1.shape
    N = B * S
    CAP = N * 2 // E
    HALF = CAP // 2
    KD = D // P
    KC = PD // P
    MH = HID // P
    PAIRS = H * DK // P
    TILES = -(-N // P)
    rows_of = [min(P, N - P * t) for t in range(TILES)]
    GB = P // S
    GT = GB * S
    GROUPS = -(-B // GB)
    tokens_of = [min(GT, N - GT * g) for g in range(GROUPS)]
    UNITS = 2 * GROUPS
    HU = H // 2
    HB = HU // 2
    NH = N // 2
    REC = D + 2
    TRASH = E * CAP
    assert KC == 2 * C and 2 * HALF == CAP and D == 2 * P and NPH * NPH + 2 == S and B * NPH <= P

    table = nc.dram_tensor("slot_table", [TRASH + 2 * N, REC], F32, kind="Internal").ap()

    with ExitStack() as ctx:
        def sb(name, shape, dt=F32):
            return ctx.enter_context(nc.sbuf_tensor(name, shape, dt))

        def sem(name):
            return ctx.enter_context(nc.semaphore(name))

        bank = [ctx.enter_context(nc.psum_tensor(f"bank{i}", [P, 512], F32)) for i in range(8)]

        xcols, imcols = KC * N, C * SIDE * IMG
        early = sb("early", [P, max(2 * PAIRS * N, imcols + xcols + KD * PD + KC * D)])
        images = early[0:B * NPH, 0:imcols].rearrange("p (c i w) -> p c i w", c=C, i=SIDE)
        patchT = early[:, imcols:imcols + xcols].rearrange("p (k n) -> p k n", k=KC)
        at = imcols + xcols
        w_in = early[:, at:at + KD * PD].rearrange("p (k n) -> p k n", k=KD)
        at += KD * PD
        w_inT = early[:, at:at + KC * D].rearrange("p (k n) -> p k n", k=KC)
        qT = early[:, 0:PAIRS * N].rearrange("p (h n) -> p h n", h=PAIRS)
        kT = early[:, PAIRS * N:2 * PAIRS * N].rearrange("p (h n) -> p h n", h=PAIRS)
        at = 2 * MH * CAP
        hidT = early[:, 0:at].rearrange("p (b m n) -> p b m n", b=2, m=MH)
        slotT = early[:, at:at + 2 * KD * CAP].rearrange("p (b k n) -> p b k n", b=2, k=KD)
        at += 2 * KD * CAP
        outT = early[:, at:at + 2 * KD * CAP].rearrange("p (b k n) -> p b k n", b=2, k=KD)
        at += 2 * KD * CAP
        y_sb = early[0:HALF, at:at + 4 * D].rearrange("p (b s d) -> p b s d", b=2, s=2)

        at = 2 * PAIRS * N
        at_slot = early[:, at:at + TILES * CAP].rearrange("p (t c) -> p t c", t=TILES)
        at += TILES * CAP
        slot_no = early[:, at:at + CAP]

        with ExitStack() as stage2:
            def split(name, scope=stage2):
                return [scope.enter_context(nc.sbuf_tensor(f"{name}_{part}", [P, KD, H * DK], F32R)) for part in ("hi", "lo")]

            wq_r, wk_r = split("wq"), split("wk")
        v_sb = sb("v_sb", [P, 3, HU * DK])
        prob = sb("prob", [P, 2, 2, HB * GT])
        probT = sb("probT", [P, 2, 2, HB * GT])
        xn2T = sb("xn2T", [P, KD * P])
        left = 4 * KD * H * DK - (3 * HU * DK + 8 * HB * GT + KD * P)
        assert left >= 0
        sb("unused", [P, left])
        wv_r = split("wv", ctx)
        wo_sb = sb("wo_sb", [P, PAIRS, D])
        wr_sb = sb("wr_sb", [P, KD, E])
        br_sb = sb("br_sb", [P, E])
        h_sb = sb("h_sb", [P, TILES, D])
        xn_sb = sb("xn_sb", [P, TILES, D])
        xnT = [sb(f"xnT_{part}", [P, KD, N], F32R) for part in ("hi", "lo")]
        zT = sb("zT", [P, PAIRS, N])
        rec = sb("rec", [P, TILES, 2, REC])
        patches = zT[0:B * NPH, :, :].rearrange("p k n -> p (k n)")[:, 0:imcols].rearrange("p (c w n) -> p c w n", c=C, w=NPH)
        w1_sb = sb("w1_sb", [P, 2, KD, HID])
        w2_sb = sb("w2_sb", [P, 2, MH, D])
        raw = [w.rearrange("p a b -> p (a b)").rearrange("p (h k n) -> p h k n", h=H, k=KD)
               for w in (w1_sb[:, 0], w1_sb[:, 1], w2_sb[:, 0])]
        raw_by_chunk = [w.rearrange("p h k n -> p k h n") for w in raw]
        assert HID == H * DK
        bias_rows = sb("bias_rows", [P, P])
        biasT = sb("biasT", [P, E * (MH + KD)])
        slots = sb("slots", [HALF, 2, 2, REC])
        slot_meta = sb("slot_meta", [HALF, E, 2, 2])
        token = sb("token", [HALF, 2, 2], U32)
        ident = sb("ident", [P, P])
        spread = sb("spread", [S, B, S])
        base = sb("base", [S, D])
        base_add = sb("base_add", [S, D])
        own = sb("own", [P, GT], BF16)
        other = sb("other", [P, HB * GT], BF16)
        before = sb("before", [P, P], BF16)
        ones = sb("ones", [P, P], BF16)
        eps = sb("eps", [P, 1])
        expert_no = sb("expert_no", [P, E])
        slot_base = sb("slot_base", [P, TILES, E])
        trash_row = sb("trash_row", [P, TILES])
        blank = sb("blank", [HALF, 2, REC])
        stats = sb("stats", [P, 6])
        mv = sb("mv", [P, 2 * TILES, 2])
        lnv = sb("lnv", [P, 2 * TILES])
        rstd0 = sb("rstd0", [P, 2 * TILES])
        newton = sb("newton", [P, 2])
        rstd = sb("rstd", [P, 2 * TILES])
        negmax = sb("negmax", [P, UNITS, HU])
        den = sb("den", [P, UNITS, HU])
        rden = sb("rden", [P, UNITS, HU])
        first_takes = sb("first_takes", [P, TILES])
        logits = sb("logits", [P, E])
        top = sb("top", [P, 8])
        topi = sb("topi", [P, 8], U32)
        topf = sb("topf", [P, 2])
        first = sb("first", [P, TILES, E])
        second = sb("second", [P, TILES, E])
        chosen = sb("chosen", [P, TILES, E], BF16)
        chosen_sum = sb("chosen_sum", [P, TILES, E], BF16)
        gap = sb("gap", [P, TILES])
        egap = sb("egap", [P, TILES])
        gsum = sb("gsum", [P, 1])
        where = sb("where", [P, E])
        kept = sb("kept", [P, E])
        picked = sb("picked", [P, E])
        row = sb("row", [P, 2])
        trash_more = sb("trash_more", [P, 2])
        more = sb("more", [P, 2])
        row_no = sb("row_no", [P, TILES, 2], U32)

        x_in = [sem(f"x_in{c}") for c in range(C)]
        w_in_in, wq_in, wk_in, wv_in, wo_in = (sem(n) for n in ("w_in_in", "wq_in", "wk_in", "wv_in", "wo_in"))
        split_hi, split_lo = sem("split_hi"), sem("split_lo")
        xnT_hi_made = sem("xnT_hi_made")
        small_in = sem("small_in")
        base_in = sem("base_in")
        w1_in = [sem(f"w1_in{i}") for i in range(2)]
        w2_in = [sem(f"w2_in{i}") for i in range(2)]
        meta_in = sem("meta_in")
        slots_in = [sem(f"slots_in{i}") for i in range(2)]
        zeroed, ident_made, patch_zeroed, const_made = (sem(n) for n in ("zeroed", "ident_made", "patch_zeroed", "const_made"))
        zeroed_dve = sem("zeroed_dve")
        base_made = sem("base_made")
        sorted_act, sorted_dve = sem("sorted_act"), sem("sorted_dve")
        filled = sem("filled")
        evac_dve, evac_act = sem("evac_dve"), sem("evac_act")
        dve_chain = sem("dve_chain")
        pool_chain = sem("pool_chain")
        act_chain = sem("act_chain")
        var_made, rstd_made = sem("var_made"), sem("rstd_made")
        xn_made, hx_made = sem("xn_made"), sem("hx_made")
        scored, maxed, exped, rden_made, prob_made = (sem(n) for n in ("scored", "maxed", "exped", "rden_made", "prob_made"))
        flipped, probT_made, z_done, z_made = (sem(n) for n in ("flipped", "probT_made", "z_done", "z_made"))
        last_filled, last_evac = sem("last_filled"), sem("last_evac")
        g_filled, g_evac = sem("g_filled"), sem("g_evac")
        rec_made, rec_copied, gap_made, egap_made, chosen_made, gates_made = (
            sem(n) for n in ("rec_made", "rec_copied", "gap_made", "egap_made", "chosen_made", "gates_made"))
        rows_made = sem("rows_made")
        at_slot_made, slot_no_made = sem("at_slot_made"), sem("slot_no_made")
        blanked = sem("blanked")
        scattered = sem("scattered")
        h2_out = sem("h2_out")
        slotT_filled, slotT_made = sem("slotT_filled"), sem("slotT_made")
        hid_filled, hid_made, out_filled, outT_made = (sem(n) for n in ("hid_filled", "hid_made", "out_filled", "outT_made"))
        y_filled, y_made, added = sem("y_filled"), sem("y_made"), sem("added")

        uses = []
        for c in range(C):
            uses.append(("w", c, "act" if c else "dve"))
            for k in (2 * c, 2 * c + 1):
                uses += [("x", (k, 0), "act"), ("x", (k, 1), "dve")]
        for t in range(TILES):
            uses += [("h", t, "act")]
            if t:
                uses += [("xn", t - 1, "dve")]
        uses += [("bias", 0, "dve")]
        assert NH <= P * (TILES - 1)
        for half in range(2):
            for p in range(PAIRS):
                uses += [("q", (p, half), "act"), ("k", (p, half), "dve")]
                if (half, p) == (0, 1):
                    uses += [("xn", TILES - 1, "dve")]
        number = {(kind, what): i for i, (kind, what, _) in enumerate(uses)}

        def emptied(i):
            eng = uses[i][2]
            return (evac_dve if eng == "dve" else evac_act), sum(u[2] == eng for u in uses[:i + 1])

        g_uses = [("v", 0), ("v", 1)]
        for i in range(UNITS):
            if i >= 6 and i % 2 == 0:
                g_uses.append(("l", (i - 6) // 2))
            if i >= 7 and i % 2:
                g_uses.append(("r", (i - 7) // 2))
            if i + 2 < UNITS:
                g_uses.append(("v", i + 2))
            if i >= 5 and i % 2 and i + 1 < UNITS:
                g_uses.append(("t", (i - 5) // 2))
            if i >= 4 and i % 2 == 0:
                g_uses.append(("o", (i - 4) // 2))
        last = TILES - 1
        assert UNITS == 2 * last + 4
        g_uses += [("t", last - 1), ("l", last - 1), ("r", last - 1)]
        g_number = {u: i for i, u in enumerate(g_uses)}
        assert len(g_number) == len(g_uses)
        last_bank = {"o": bank[0], "t": bank[1], "l": bank[2], "r": bank[3]}
        G = bank[7]
        Z = bank[6]

        def g_bank(what):
            return G if what in g_number else last_bank[what[0]]


        def span(i):
            return GT * (i // 2), tokens_of[i // 2], i % 2

        def patch_cols(dst, k, part):
            v = dst[:, k, :].rearrange("p (b s) -> p b s", s=S)[:, :, 2:S]
            return v.rearrange("p b (f w) -> p w b f", w=NPH)[:, 3 * part:3 * part + 3]

        def pixels(c, part):
            src = images[:, c].rearrange("p i (w j) -> p w i j", j=SIDE)[:, 3 * part:3 * part + 3]
            return patches[:, c, 3 * part:3 * part + 3, :].rearrange("p w (i j) -> p w i j", i=SIDE), src

        block = ctx.enter_context(nc.Block())

        @block.sync
        def _(sp):
            for c in range(C):
                sp.dma_start(images[:, c], x[:, c].rearrange("b (f i) w -> b f (i w)", i=SIDE)).then_inc(x_in[c], 16)
            sp.dma_start(base[1:S, :], pos[0]).then_inc(base_in, 16)
            sp.dma_start(base[0:1, :], cls_tok[0]).then_inc(base_in, 16)
            sp.dma_start(base_add[1:2, :], tok_cls[0]).then_inc(base_in, 16)
            sp.dma_start(base_add[2:S, :], tok_b.rearrange("(a d) -> a d", a=1).to_broadcast([S - 2, D])).then_inc(base_in, 16)
            for w, dst, done in ((wq, raw[0], wq_in), (wk, raw[1], wk_in), (wv, raw[2], wv_in)):
                sp.dma_start(dst, w.rearrange("h (p k) n -> p h k n", k=KD)).then_inc(done, 16)
            sp.dma_start(bias_rows[0:E * MH, :], b1.rearrange("e (m p) -> (e m) p", p=P)).then_inc(small_in, 16)
            sp.dma_start(bias_rows[E * MH:E * (MH + KD), :], b2.rearrange("e (m p) -> (e m) p", p=P)).then_inc(small_in, 16)
            sp.dma_start(wr_sb[:, :, :], wr.rearrange("(k p) e -> p k e", p=P)).then_inc(small_in, 16)
            sp.dma_start(br_sb[:, :], br.rearrange("(a e) -> a e", a=1).to_broadcast([P, E])).then_inc(small_in, 16)
            sp.dma_start(wo_sb[:, :, :], wo.rearrange("(t p) d -> p t d", p=P)).then_inc(wo_in, 16)
            sp.wait_ge(const_made, 1)
            for s in range(2):
                sp.dma_start(table[0:TRASH, :].rearrange("(e s p) c -> s p e c", p=HALF, s=2)[s],
                             blank[:, s:s + 1, :].to_broadcast([HALF, E, REC])).then_inc(blanked, 16)
            sp.dma_start(out[N:N + CAP, :].rearrange("(s p) d -> p s d", p=HALF), blank[:, :, 0:D]).then_inc(h2_out, 16)
            sp.wait_ge(split_lo, 3)
            for e in range(2):
                sp.dma_start(w1_sb[:, e], w1[e].rearrange("(k p) n -> p k n", p=P)).then_inc(w1_in[e], 16)
                sp.dma_start(w2_sb[:, e], w2[e].rearrange("(m p) n -> p m n", p=P)).then_inc(w2_in[e], 16)
            for t in range(TILES):
                sp.wait_ge(var_made, TILES + t + 1)
                sp.dma_start(out[P * t:P * t + rows_of[t], :], h_sb[0:rows_of[t], t, :]).then_inc(h2_out, 16)

            def load_slots(e, b):
                src = table[bass.ds(e * CAP, CAP), :].rearrange("(s p) c -> p s c", p=HALF)
                sp.dma_start(slots[:, b], src).then_inc(slots_in[b], 16)

            sp.wait_ge(scattered, 16 * 2 * TILES)
            load_slots(1, 1)
            sp.dma_start(slot_meta[:, :, :, :], table[0:TRASH, D:REC].rearrange("(e s p) c -> p e s c", p=HALF, s=2)).then_inc(meta_in, 16)

            def refill(e, b):
                sp.wait_ge(slotT_filled, e + 1)
                load_slots(e + 2, b)
                sp.wait_ge(hid_filled, MH // 2 * (e + 1))
                sp.dma_start(w1_sb[:, b], w1[bass.ds(e + 2, 1)].rearrange("a (k p) n -> p (a k) n", p=P)).then_inc(w1_in[b], 16)
                sp.wait_ge(out_filled, e + 1)
                sp.dma_start(w2_sb[:, b], w2[bass.ds(e + 2, 1)].rearrange("a (m p) n -> p (a m) n", p=P)).then_inc(w2_in[b], 16)

            with sp.Fori(0, E - 3, 2) as e:
                refill(e, 0)
                refill(e + 1, 1)
            sp.wait_ge(h2_out, 16 * (TILES + 1))
            sp.wait_ge(added, 32 * E)

        @block.gpsimd
        def _(pool):
            count = [0]

            def chained(ins):
                count[0] += 1
                ins.then_inc(pool_chain, 1)
                pool.wait_ge(pool_chain, count[0])

            nc.gpsimd.memset(ident[:, :], 0.0).then_inc(zeroed, 1)
            pool.wait_ge(zeroed, 1)
            nc.gpsimd.affine_select(out=ident[:, :], in_=ident[:, :], compare_op=ALU.not_equal, fill=1.0, base=0,
                                    pattern=[[1, P]], channel_multiplier=-1).then_inc(ident_made, 1)
            nc.gpsimd.memset(patchT[:, :, :].rearrange("p k (b s) -> p (k b) s", s=S)[:, :, 0:2], 0.0).then_inc(patch_zeroed, 1)
            chained(nc.gpsimd.memset(spread[:, :, :], 0.0))
            chained(nc.gpsimd.affine_select(out=spread[:, :, :], in_=spread[:, :, :], compare_op=ALU.not_equal, fill=1.0,
                                            base=0, pattern=[[0, B], [1, S]], channel_multiplier=-1))
            nc.gpsimd.memset(eps[:, :], EPS)
            for lo in (0, P // 2):
                o3 = own[lo:lo + GB, :].rearrange("p (a s) -> p a s", s=S)
                m3 = other[lo:lo + GB, :].rearrange("p (h a s) -> p h a s", a=GB, s=S)
                chained(nc.gpsimd.memset(o3, 0.0))
                chained(nc.gpsimd.affine_select(out=o3, in_=o3, compare_op=ALU.not_equal, fill=1.0, base=0,
                                                pattern=[[1, GB], [0, S]], channel_multiplier=-1))
                chained(nc.gpsimd.memset(m3, MASKED))
                chained(nc.gpsimd.affine_select(out=m3, in_=m3, compare_op=ALU.not_equal, fill=0.0, base=0,
                                                pattern=[[0, HB], [1, GB], [0, S]], channel_multiplier=-1))
            chained(nc.gpsimd.memset(ones[:, :], 1.0))
            chained(nc.gpsimd.affine_select(out=before[:, :], in_=ones[:, :], compare_op=ALU.is_ge, fill=0.0, base=-1,
                                            pattern=[[1, P]], channel_multiplier=-1))
            nc.gpsimd.iota(expert_no[:, :], pattern=[[1, E]], base=0, channel_multiplier=0,
                           allow_small_or_imprecise_dtypes=True)
            nc.gpsimd.iota(slot_base[:, :, :], pattern=[[-P, TILES], [CAP, E]], base=-TRASH, channel_multiplier=-1,
                           allow_small_or_imprecise_dtypes=True)
            nc.gpsimd.iota(trash_row[:, :], pattern=[[P, TILES]], base=TRASH, channel_multiplier=1,
                           allow_small_or_imprecise_dtypes=True)
            nc.gpsimd.iota(trash_more[:, :], pattern=[[N, 2]], base=0, channel_multiplier=0,
                           allow_small_or_imprecise_dtypes=True)
            nc.gpsimd.iota(rec[:, :, :, D].bitcast(I32), pattern=[[P, TILES], [0, 2]], base=0, channel_multiplier=1)
            chained(nc.gpsimd.memset(blank[:, :, :], 0.0))
            chained(nc.gpsimd.iota(blank[:, :, D].bitcast(I32), pattern=[[HALF, 2]], base=N, channel_multiplier=1))
            nc.gpsimd.memset(chosen_sum[:, 0, :], 0.0).then_inc(const_made, 1)

            def residual(t):
                r = rows_of[t]
                pool.wait_ge(xn_made, t + 1)
                nc.gpsimd.tensor_tensor(h_sb[0:r, t, :], h_sb[0:r, t, :], xn_sb[0:r, t, :], ALU.add).then_inc(hx_made, 1)

            for n, w in enumerate((wq_r, wk_r, wv_r)):
                pool.wait_ge(split_hi, n + 1)
                lo, hi = (part[:, :, :].rearrange("p k (h n) -> p k h n", h=H) for part in (w[1], w[0]))
                nc.gpsimd.tensor_tensor(lo, raw_by_chunk[n], hi.bitcast(F32), ALU.subtract).then_inc(split_lo, 1)
            for t in range(TILES):
                residual(t)
            nc.gpsimd.iota(slot_no, pattern=[[1, CAP]], base=0, channel_multiplier=0,
                           allow_small_or_imprecise_dtypes=True).then_inc(slot_no_made, 1)

            def normalise(i):
                _, T, b = span(i)
                for par in range(2):
                    pool.wait_ge(rden_made, 2 * i + par + 1)
                    v = prob[0:T, b, par, 0:HB * T].rearrange("p (h m) -> p h m", h=HB)
                    r = rden[0:T, i, HB * par:HB * par + HB].rearrange("p (h a) -> p h a", a=1).to_broadcast([T, HB, T])
                    nc.gpsimd.tensor_tensor(v, v, r, ALU.mult).then_inc(prob_made, 1)

            def scatter(t):
                r = rows_of[t]
                if t == 0:
                    pool.wait_ge(blanked, 32)
                pool.wait_ge(rec_copied, t + 1)
                pool.wait_ge(gates_made, t + 1)
                pool.wait_ge(rows_made, t + 1)
                for k in range(2):
                    pool.indirect_dma_start(
                        table, bass.IndirectOffsetOnAxis(ap=row_no[0:r, t, k:k + 1], axis=0),
                        rec[0:r, t, k, :], None).then_inc(scattered, 16)

            for i in range(UNITS):
                normalise(i)
                if i >= 8 and i % 2 == 0:
                    scatter((i - 8) // 2)
            for t in range(last - 2, TILES):
                scatter(t)

            pool.wait_ge(h2_out, 16 * (TILES + 1))
            for e in range(E):
                pool.wait_ge(y_made, e + 1)
                if e:
                    pool.wait_ge(added, 32 * e)
                for s in range(2):
                    pool.indirect_dma_start(
                        out, bass.IndirectOffsetOnAxis(ap=token[:, e % 2, s:s + 1], axis=0),
                        y_sb[:, e % 2, s, :], None, compute_op=ALU.add).then_inc(added, 16)

        @block.scalar
        def _(act):
            nc.scalar.preload_act_table_set("natural_log_exp_and_others")
            act.dma_start(w_in[:, :, :], tok_w.rearrange("(k p) n -> p k n", p=P)).then_inc(w_in_in, 16)

            count = [0]

            def chained(ins):
                count[0] += 1
                ins.then_inc(act_chain, 1)
                act.wait_ge(act_chain, count[0])

            def patches_out(k, part):
                i = number["x", (k, part)]
                act.wait_ge(filled, i + 1)
                src = bank[i % 8][:, 0:3 * B * NPH].rearrange("p (w b f) -> p w b f", w=3, b=B)
                nc.scalar.copy(patch_cols(patchT, k, part), src).then_inc(evac_act, 1)

            def sort(c):
                act.wait_ge(x_in[c], 16)
                nc.scalar.copy(*pixels(c, 0)).then_inc(sorted_act, 1)

            sort(0)
            sort(1)
            act.wait_ge(patch_zeroed, 1)
            for c in range(C):
                if c:
                    i = number["w", c]
                    act.wait_ge(filled, i + 1)
                    nc.scalar.copy(w_inT[:, 2 * c:2 * c + 2, :], bank[i % 8][:, 0:2 * D].rearrange("p (k n) -> p k n", k=2)).then_inc(evac_act, 1)
                patches_out(2 * c, 0)
                patches_out(2 * c + 1, 0)
                if c + 2 < C:
                    sort(c + 2)

            def rstd_guess(j, r):
                act.wait_ge(var_made, j + 1)
                chained(nc.scalar.activation(lnv[0:r, j:j + 1], mv[0:r, j, 1:2], ACT.Ln, bias=eps[0:r, :]))
                nc.scalar.activation(rstd0[0:r, j:j + 1], lnv[0:r, j:j + 1], ACT.Exp, scale=-0.5).then_inc(rstd_made, 1)

            def h_out(t):
                i = number["h", t]
                r = rows_of[t]
                act.wait_ge(filled, i + 1)
                nc.scalar.copy(h_sb[0:r, t, :], bank[i % 8][0:r, 0:D]).then_inc(evac_act, 1)

            def round_weights(n):
                act.wait_ge((wq_in, wk_in, wv_in)[n], 16)
                hi = (wq_r, wk_r, wv_r)[n][0][:, :, :].rearrange("p k (h n) -> p k h n", h=H)
                nc.scalar.copy(hi, raw_by_chunk[n]).then_inc(split_hi, 1)

            def xnT_hi_out(t):
                i, r = number["xn", t], rows_of[t]
                act.wait_ge(filled, i + 1)
                nc.scalar.copy(xnT[0][:, :, P * t:P * t + r], bank[i % 8][:, 0:KD * r].rearrange("p (k n) -> p k n", k=KD)).then_inc(xnT_hi_made, 1)

            round_weights(0)
            act.wait_ge(const_made, 1)
            for t in range(TILES):
                h_out(t)
                rstd_guess(t, rows_of[t])
                if t in (0, 1):
                    round_weights(1 + t)
                if t:
                    xnT_hi_out(t - 1)
            for half in range(2):
                for p in range(PAIRS):
                    i = number["q", (p, half)]
                    act.wait_ge(filled, i + 1)
                    nc.scalar.mul(qT[:, p, NH * half:NH * half + NH], bank[i % 8][:, 0:NH], float(DK) ** -0.5).then_inc(evac_act, 1)
                    if (half, p) == (0, 1):
                        xnT_hi_out(TILES - 1)

            def exponentials(i):
                _, T, b = span(i)
                for par in range(2):
                    act.wait_ge(maxed, 2 * i + par + 1)
                    if i >= 2:
                        act.wait_ge(flipped, 2 * (i - 2) + par + 1)
                    for h in range(HB):
                        j = HB * par + h
                        ins = nc.scalar.activation(prob[0:T, b, par, h * T:h * T + T], bank[2 * b + par][0:T, h * T:h * T + T],
                                                   ACT.Exp, bias=negmax[0:T, i, j:j + 1], accum_out=den[0:T, i, j:j + 1])
                    ins.then_inc(exped, 1)

            def z_out(i):
                o, T, _ = span(i)
                act.wait_ge(z_done, i + 1)
                nc.scalar.copy(zT[:, HB * (i % 2):HB * (i % 2) + HB, o:o + T],
                               Z[:, 0:HB * T].rearrange("p (h n) -> p h n", h=HB)).then_inc(z_made, 1)

            def gate_exp(t):
                r = rows_of[t]
                act.wait_ge(gap_made, t + 1)
                nc.scalar.activation(egap[0:r, t:t + 1], gap[0:r, t:t + 1], ACT.Exp).then_inc(egap_made, 1)

            def second_record(t):
                r = rows_of[t]
                act.wait_ge(rec_made, t + 1)
                nc.scalar.copy(rec[0:r, t, 1, 0:D], rec[0:r, t, 0, 0:D]).then_inc(rec_copied, 1)

            exponentials(0)
            for i in range(UNITS):
                if i >= 5 and i % 2:
                    rstd_guess(TILES + (i - 5) // 2, rows_of[(i - 5) // 2])
                if i >= 1:
                    z_out(i - 1)
                if i + 1 < UNITS:
                    exponentials(i + 1)
                if i >= 7 and i % 2:
                    gate_exp((i - 7) // 2)
                if i >= 5 and i % 2:
                    second_record((i - 5) // 2)
            z_out(UNITS - 1)
            gate_exp(last - 1)
            rstd_guess(TILES + last, rows_of[last])
            second_record(last)
            gate_exp(last)

            def gelu(e, b):
                for j in range(MH // 2):
                    act.wait_ge(hid_filled, MH // 2 * e + j + 1)
                    for m in (2 * j, 2 * j + 1):
                        bias = biasT[:, bass.ds(e * MH + m, 1)]
                        ins = nc.scalar.activation(hidT[:, b, m, :], bank[j][:, (m % 2) * CAP:(m % 2) * CAP + CAP], ACT.Gelu, bias=bias)
                    ins.then_inc(hid_made, 1)

            nc.scalar.preload_act_table(ACT.Gelu)
            act.wait_ge(slotT_filled, 1)
            for k in range(KD):
                ins = nc.scalar.copy(slotT[:, 0, k, :], bank[4 + k][:, 0:CAP])
            ins.then_inc(slotT_made, 1)
            gelu(0, 0)
            gelu(1, 1)
            with act.Fori(2, E - 1, 2) as e:
                act.wait_ge(out_filled, e - 1)
                gelu(e, 0)
                act.wait_ge(out_filled, e)
                gelu(e + 1, 1)

        @block.vector
        def _(dve):
            count = [0]

            def chained(ins):
                count[0] += 1
                ins.then_inc(dve_chain, 1)
                dve.wait_ge(dve_chain, count[0])

            chained(nc.vector.memset(base_add[0:1, :], 0.0))
            def sort(c):
                dve.wait_ge(x_in[c], 16)
                nc.vector.tensor_copy(*pixels(c, 1)).then_inc(sorted_dve, 1)

            sort(0)
            sort(1)
            dve.wait_ge(patch_zeroed, 1)
            for c in range(C):
                if c == 0:
                    i = number["w", c]
                    dve.wait_ge(filled, i + 1)
                    nc.vector.tensor_copy(w_inT[:, 0:2, :], bank[i % 8][:, 0:2 * D].rearrange("p (k n) -> p k n", k=2)).then_inc(evac_dve, 1)
                for k in (2 * c, 2 * c + 1):
                    i = number["x", (k, 1)]
                    dve.wait_ge(filled, i + 1)
                    src = bank[i % 8][:, 0:3 * B * NPH].rearrange("p (w b f) -> p w b f", w=3, b=B)
                    nc.vector.tensor_copy(patch_cols(patchT, k, 1), src).then_inc(evac_dve, 1)
                if c + 2 < C:
                    sort(c + 2)
            dve.wait_ge(base_in, 64)
            nc.vector.tensor_tensor(base[:, :], base[:, :], base_add[:, :], ALU.add).then_inc(base_made, 1)

            def variance(src, j, r):
                chained(nc.vector.bn_stats(stats[0:r, :], src))
                nc.vector.bn_aggr(mv[0:r, j, :], stats[0:r, :]).then_inc(var_made, 1)

            def layernorm(dst, src, j, r):
                dve.wait_ge(rstd_made, j + 1)
                chained(nc.vector.tensor_tensor(newton[0:r, 0:1], rstd0[0:r, j:j + 1], rstd0[0:r, j:j + 1], ALU.mult))
                chained(nc.vector.scalar_tensor_tensor(out=newton[0:r, 1:2], in0=mv[0:r, j, 1:2], scalar=EPS,
                                                       in1=newton[0:r, 0:1], op0=ALU.add, op1=ALU.mult))
                chained(nc.vector.tensor_scalar(newton[0:r, 0:1], newton[0:r, 1:2], -0.5, 1.5, ALU.mult, ALU.add))
                chained(nc.vector.tensor_tensor(rstd[0:r, j:j + 1], newton[0:r, 0:1], rstd0[0:r, j:j + 1], ALU.mult))
                return nc.vector.tensor_scalar(dst, src, mv[0:r, j, 0:1], rstd[0:r, j:j + 1], ALU.subtract, ALU.mult)

            def xnT_lo_out(t):
                i, r = number["xn", t], rows_of[t]
                dve.wait_ge(xnT_hi_made, t + 1)
                src = bank[i % 8][:, 0:KD * r].rearrange("p (k n) -> p k n", k=KD)
                nc.vector.tensor_tensor(xnT[1][:, :, P * t:P * t + r], src, xnT[0][:, :, P * t:P * t + r].bitcast(F32),
                                        ALU.subtract).then_inc(evac_dve, 1)

            for t in range(TILES):
                r = rows_of[t]
                sem_, value = emptied(number["h", t])
                dve.wait_ge(sem_, value)
                variance(h_sb[0:r, t, :], t, r)
                layernorm(xn_sb[0:r, t, :], h_sb[0:r, t, :], t, r).then_inc(xn_made, 1)
                if t:
                    xnT_lo_out(t - 1)
            i = number["bias", 0]
            dve.wait_ge(filled, i + 1)
            nc.vector.tensor_copy(biasT[:, :], bank[i % 8][:, 0:E * (MH + KD)]).then_inc(evac_dve, 1)
            for half in range(2):
                for p in range(PAIRS):
                    i = number["k", (p, half)]
                    dve.wait_ge(filled, i + 1)
                    nc.vector.tensor_copy(kT[:, p, NH * half:NH * half + NH], bank[i % 8][:, 0:NH]).then_inc(evac_dve, 1)
                    if (half, p) == (0, 1):
                        xnT_lo_out(TILES - 1)

            def row_max(i):
                _, T, b = span(i)
                for par in range(2):
                    dve.wait_ge(scored, 2 * i + par + 1)
                    nc.vector.tensor_reduce(negmax[0:T, i, HB * par:HB * par + HB],
                                            bank[2 * b + par][0:T, 0:HB * T].rearrange("p (h m) -> p h m", h=HB),
                                            AX.X, ALU.max, negate=True).then_inc(maxed, 1)

            def row_rden(i):
                _, T, _ = span(i)
                for par in range(2):
                    dve.wait_ge(exped, 2 * i + par + 1)
                    nc.vector.reciprocal(rden[0:T, i, HB * par:HB * par + HB], den[0:T, i, HB * par:HB * par + HB]).then_inc(rden_made, 1)

            def probT_out(i):
                _, T, b = span(i)
                for par in range(2):
                    dve.wait_ge(flipped, 2 * i + par + 1)
                    if i >= 2:
                        dve.wait_ge(z_done, i - 1)
                    nc.vector.tensor_copy(probT[0:T, b, par, 0:HB * T], bank[4 + par][0:T, 0:HB * T]).then_inc(probT_made, 1)

            last_step = {"o": 1, "t": 2, "l": 3, "r": 4}

            def g_ready(what):
                if what in g_number:
                    dve.wait_ge(g_filled, g_number[what] + 1)
                else:
                    dve.wait_ge(last_filled, last_step[what[0]])

            def g_read(what, ins):
                if what in g_number:
                    ins.then_inc(g_evac, 1)
                    dve.wait_ge(g_evac, g_number[what] + 1)
                else:
                    ins.then_inc(last_evac, 1)
                    dve.wait_ge(last_evac, last_step[what[0]])

            def v_out(i):
                _, T, _ = span(i)
                g_ready(("v", i))
                if i >= 3:
                    dve.wait_ge(z_done, i - 2)
                nc.vector.tensor_copy(v_sb[0:T, i % 3, :], G[0:T, :]).then_inc(g_evac, 1)

            def h2_of(t):
                r = rows_of[t]
                what = ("o", t)
                g_ready(what)
                dve.wait_ge(hx_made, t + 1)
                g_read(what, nc.vector.tensor_tensor(h_sb[0:r, t, :], h_sb[0:r, t, :], g_bank(what)[0:r, 0:D], ALU.add))
                chained(nc.vector.bn_stats(stats[0:r, :], h_sb[0:r, t, :]))
                nc.vector.bn_aggr(mv[0:r, TILES + t, :], stats[0:r, :]).then_inc(var_made, 1)

            def second_layernorm(t):
                r = rows_of[t]
                layernorm(rec[0:r, t, 0, 0:D], h_sb[0:r, t, :], TILES + t, r).then_inc(rec_made, 1)

            def xn2T_out(t):
                r = rows_of[t]
                what = ("t", t)
                g_ready(what)
                g_read(what, nc.vector.tensor_copy(xn2T[:, 0:KD * r], g_bank(what)[:, 0:KD * r]))

            def logits_out(t):
                r = rows_of[t]
                what = ("l", t)
                g_ready(what)
                g_read(what, nc.vector.tensor_tensor(logits[0:r, :], g_bank(what)[0:r, 0:E], br_sb[0:r, :], ALU.add))

            def choose(t):
                r = rows_of[t]
                chained(nc.vector.max(top[0:r, :], logits[0:r, :]))
                nc.vector.tensor_tensor(gap[0:r, t:t + 1], top[0:r, 1:2], top[0:r, 0:1], ALU.subtract).then_inc(gap_made, 1)
                chained(nc.vector.max_index(topi[0:r, :], top[0:r, :], logits[0:r, :]))
                chained(nc.vector.tensor_copy(topf[0:r, :], topi[0:r, 0:2]))
                nc.vector.tensor_scalar(second[0:r, t, :], expert_no[0:r, :], topf[0:r, 1:2], None, ALU.is_equal)
                chained(nc.vector.tensor_scalar(first[0:r, t, :], expert_no[0:r, :], topf[0:r, 0:1], None, ALU.is_equal))
                nc.vector.tensor_tensor(chosen[0:r, t, :], first[0:r, t, :], second[0:r, t, :], ALU.add).then_inc(chosen_made, 1)
                chained(nc.vector.tensor_tensor(first_takes[0:r, t:t + 1], first[0:r, t, 0:1], second[0:r, t, 0:1], ALU.add))
                dve.wait_ge(chosen_made, t + 1)
                if t < last:
                    chained(nc.vector.tensor_tensor(chosen_sum[:, t + 1, :], chosen_sum[:, t, :], chosen[:, t, :], ALU.add))

            def gates(t):
                r = rows_of[t]
                dve.wait_ge(egap_made, t + 1)
                chained(nc.vector.tensor_scalar(gsum[0:r, :], egap[0:r, t:t + 1], 1.0, None, ALU.add))
                chained(nc.vector.reciprocal(rec[0:r, t, 0, D + 1:D + 2], gsum[0:r, :]))
                nc.vector.tensor_tensor(rec[0:r, t, 1, D + 1:D + 2], rec[0:r, t, 0, D + 1:D + 2], egap[0:r, t:t + 1],
                                        ALU.mult).then_inc(gates_made, 1)

            def ranks_out(t):
                r = rows_of[t]
                what = ("r", t)
                g_ready(what)
                rank = g_bank(what)[0:r, 0:E]
                nc.vector.tensor_scalar(at_slot[0:r, t, :], slot_no[0:r, :], rank[:, 0:1], first_takes[0:r, t:t + 1],
                                        ALU.is_equal, ALU.mult).then_inc(at_slot_made, 1)
                chained(nc.vector.tensor_tensor(where[0:r, :], rank, slot_base[0:r, t, :], ALU.add))
                g_read(what, nc.vector.scalar_tensor_tensor(out=kept[0:r, :], in0=rank, scalar=float(CAP), in1=where[0:r, :],
                                                            op0=ALU.is_lt, op1=ALU.mult))

            def rows_out(t):
                r = rows_of[t]
                for k, hot in enumerate((first, second)):
                    chained(nc.vector.tensor_tensor_reduce(picked[0:r, :], hot[0:r, t, :], kept[0:r, :], 1.0, 0.0,
                                                           ALU.mult, ALU.add, row[0:r, k:k + 1]))
                chained(nc.vector.scalar_tensor_tensor(out=more[0:r, :], in0=row[0:r, :], scalar=0.0, in1=trash_more[0:r, :],
                                                       op0=ALU.is_equal, op1=ALU.mult))
                nc.vector.scalar_tensor_tensor(out=row_no[0:r, t, :], in0=row[0:r, :], scalar=trash_row[0:r, t:t + 1],
                                               in1=more[0:r, :], op0=ALU.add, op1=ALU.add).then_inc(rows_made, 1)

            dve.wait_ge(small_in, 64)
            dve.wait_ge(slot_no_made, 1)
            dve.wait_ge(const_made, 1)
            v_out(0)
            row_max(0)
            v_out(1)
            for i in range(UNITS):
                row_rden(i)
                if i >= 5 and i % 2:
                    h2_of((i - 5) // 2)
                if i + 1 < UNITS:
                    row_max(i + 1)
                if i >= 7 and i % 2:
                    ranks_out((i - 7) // 2)
                if i == UNITS - 1:
                    probT_out(i)
                if i >= 5 and i % 2:
                    second_layernorm((i - 5) // 2)
                if i >= 6 and i % 2 == 0:
                    logits_out((i - 6) // 2)
                if i + 2 < UNITS:
                    v_out(i + 2)
                if i < UNITS - 1:
                    probT_out(i)
                if i >= 5 and i % 2:
                    xn2T_out((i - 5) // 2)
                if i >= 6 and i % 2 == 0:
                    choose((i - 6) // 2)
                if i >= 7 and i % 2:
                    rows_out((i - 7) // 2)
                    if i < UNITS - 1:
                        gates((i - 7) // 2)
            logits_out(last - 1)
            choose(last - 1)
            h2_of(last)
            ranks_out(last - 1)
            second_layernorm(last)
            gates(last - 2)
            xn2T_out(last)
            rows_out(last - 1)
            logits_out(last)
            choose(last)
            gates(last - 1)
            ranks_out(last)
            rows_out(last)
            gates(last)

            def slotT_out(e, b):
                dve.wait_ge(slotT_filled, e + 1)
                nc.vector.tensor_copy(slotT[:, b], bank[7][:, 0:KD * CAP].rearrange("p (k n) -> p k n", k=KD)).then_inc(slotT_made, 1)

            def outT_out(e, b):
                dve.wait_ge(out_filled, e + 1)
                for d in range(KD):
                    ins = nc.vector.tensor_scalar(outT[:, b, d, :], bank[4 + d][:, 0:CAP],
                                                  biasT[:, bass.ds(E * MH + e * KD + d, 1)], None, ALU.add)
                ins.then_inc(outT_made, 1)

            def y_out(e, b):
                dve.wait_ge(y_filled, e + 1)
                nc.vector.tensor_copy(token[:, b, :], slot_meta[:, bass.ds(e, 1), :, 0:1].rearrange("p a s c -> p (a s c)").bitcast(U32))
                for s in range(2):
                    ins = nc.vector.tensor_scalar(y_sb[:, b, s, :], bank[6][0:HALF, s * D:s * D + D],
                                                  slot_meta[:, bass.ds(e, 1), s, 1:2].rearrange("p a c -> p (a c)"), None, ALU.mult)
                ins.then_inc(y_made, 1)

            def mid(e, b):
                y_out(e - 1, 1 - b)
                slotT_out(e + 1, 1 - b)
                outT_out(e, b)

            slotT_out(1, 1)
            outT_out(0, 0)
            dve.wait_ge(meta_in, 16)
            mid(1, 1)
            mid(2, 0)
            with dve.Fori(3, E - 2, 2) as e:
                dve.wait_ge(added, 32 * (e - 2))
                mid(e, 1)
                dve.wait_ge(added, 32 * (e - 1))
                mid(e + 1, 0)
            dve.wait_ge(added, 32 * (E - 3))
            y_out(E - 2, 0)
            outT_out(E - 1, 1)
            dve.wait_ge(added, 32 * (E - 2))
            y_out(E - 1, 1)

        @block.tensor
        def _(pe):
            def free(i):
                if i >= 8:
                    s, v = emptied(i - 8)
                    pe.wait_ge(s, v)

            def warm(n, spare):
                for _ in range(n):
                    pe.matmul(spare[:, 0:P], ident[:, :], ident[:, :], start=True, stop=True)

            pe.wait_ge(ident_made, 1)
            warm(9, bank[7])
            pe.wait_ge(w_in_in, 16)
            for c in range(C):
                i = number["w", c]
                free(i)
                for k in (2 * c, 2 * c + 1):
                    for m in range(KD):
                        o = (k % 2) * D + m * P
                        mm = pe.transpose(bank[i % 8][:, o:o + P], w_in[:, m, k * P:(k + 1) * P], ident[:, :])
                mm.then_inc(filled, 1)
                pe.wait_ge(sorted_act, c + 1)
                pe.wait_ge(sorted_dve, c + 1)
                for k in (2 * c, 2 * c + 1):
                    for part in range(2):
                        i = number["x", (k, part)]
                        free(i)
                        for w in range(3):
                            src = patches[:, c, 3 * part + w, P * (k % 2):P * (k % 2) + P]
                            mm = pe.transpose(bank[i % 8][:, w * B * NPH:(w + 1) * B * NPH], src, ident[0:B * NPH, 0:B * NPH])
                        mm.then_inc(filled, 1)
            pe.wait_ge(base_made, 1)
            pe.wait_ge(const_made, 1)
            for s, v in (emptied(number["x", (KC - 1, 0)]), emptied(number["x", (KC - 1, 1)])):
                pe.wait_ge(s, v)
            spread_v = spread[:, :, :].rearrange("s b t -> s (b t)")

            def embed(t):
                i, r = number["h", t], rows_of[t]
                free(i)
                for k in range(KC):
                    pe.matmul(bank[i % 8][0:r, 0:D], patchT[:, k, P * t:P * t + r], w_inT[:, k, :], start=(k == 0), stop=False)
                pe.matmul(bank[i % 8][0:r, 0:D], spread_v[:, P * t:P * t + r], base[:, :], start=False, stop=True).then_inc(filled, 1)

            def flip_xn(t):
                i, r = number["xn", t], rows_of[t]
                free(i)
                pe.wait_ge(xn_made, t + 1)
                for k in range(KD):
                    mm = pe.transpose(bank[i % 8][:, k * r:k * r + r], xn_sb[0:r, t, :].rearrange("p (m k) -> p k m", k=KD)[:, k, :], ident[0:r, 0:r])
                mm.then_inc(filled, 1)

            for t in range(TILES):
                embed(t)
                if t:
                    flip_xn(t - 1)
            i = number["bias", 0]
            free(i)
            pe.wait_ge(small_in, 64)
            pe.transpose(bank[i % 8][:, 0:E * (MH + KD)], bias_rows[0:E * (MH + KD), :],
                         ident[0:E * (MH + KD), 0:E * (MH + KD)]).then_inc(filled, 1)

            def split_product(out_, lhs, rhs):
                terms = [(a, b, k) for a, b in ((0, 0), (0, 1), (1, 0)) for k in range(KD)]
                for n, (a, b, k) in enumerate(terms):
                    mm = pe.matmul(out_, lhs[a](k), rhs[b](k), start=(n == 0), stop=(n == len(terms) - 1))
                return mm

            s, v = emptied(number["xn", (NH - 1) // P])
            pe.wait_ge(s, v)
            for half in range(2):
                for p in range(PAIRS):
                    for n, (name, w) in enumerate((("q", wq_r), ("k", wk_r))):
                        i = number[name, (p, half)]
                        free(i)
                        pe.wait_ge(split_lo, n + 1)
                        split_product(bank[i % 8][:, 0:NH],
                                      [lambda k, part=part: part[:, k, 2 * DK * p:2 * DK * (p + 1)] for part in w],
                                      [lambda k, part=part: part[:, k, NH * half:NH * half + NH] for part in xnT]).then_inc(filled, 1)
                    if (half, p) == (0, 1):
                        flip_xn(TILES - 1)
                if half == 0:
                    s, v = emptied(number["xn", TILES - 1])
                    pe.wait_ge(s, v)

            def g_free(what):
                if what in g_number:
                    if g_number[what]:
                        pe.wait_ge(g_evac, g_number[what])
                elif what[0] == "o":
                    pe.wait_ge(exped, 2 * UNITS)
                else:
                    pe.wait_ge(last_evac, "otlr".index(what[0]))

            def g_signal(what, mm):
                mm.then_inc(g_filled if what in g_number else last_filled, 1)

            def values(i):
                o, T, _ = span(i)
                g_free(("v", i))
                c = HU * DK * (i % 2)
                split_product(G[0:T, :], [lambda k, part=part: part[:, k, o:o + T] for part in xnT],
                              [lambda k, part=part: part[:, k, c:c + HU * DK] for part in wv_r]).then_inc(g_filled, 1)

            def scores(i):
                o, T, b = span(i)
                if i >= 2:
                    pe.wait_ge(exped, 2 * (i - 1))
                masked = T > S
                if masked:
                    for par in range(2):
                        lo = par * (P // 2)
                        pe.matmul(bank[2 * b + par][0:T, 0:HB * T], own[lo:lo + GB, :], other[lo:lo + GB, :],
                                  start=True, stop=False)
                for h in range(HB):
                    for par in range(2):
                        lo, p = par * (P // 2), HB * (i % 2) + h
                        mm = pe.matmul(bank[2 * b + par][0:T, h * T:h * T + T], qT[lo:lo + DK, p, o:o + T], kT[lo:lo + DK, p, o:o + T],
                                       start=not masked, stop=(h == HB - 1 or not masked))
                        if h == HB - 1:
                            mm.then_inc(scored, 1)

            def flip(i):
                _, T, b = span(i)
                for par in range(2):
                    pe.wait_ge(prob_made, 2 * i + par + 1)
                    if i >= 1:
                        pe.wait_ge(probT_made, 2 * (i - 1) + par + 1)
                    for h in range(HB):
                        mm = pe.transpose(bank[4 + par][0:T, h * T:h * T + T], prob[0:T, b, par, h * T:h * T + T], ident[0:T, 0:T])
                    mm.then_inc(flipped, 1)

            def weigh(i):
                _, T, b = span(i)
                pe.wait_ge(probT_made, 2 * i + 2)
                pe.wait_ge(g_evac, g_number["v", i] + 1)
                if i >= 1:
                    pe.wait_ge(z_made, i)
                for h in range(HB):
                    for par in range(2):
                        lo, c = par * (P // 2), (2 * h + par) * DK
                        mm = pe.matmul(Z[lo:lo + DK, h * T:h * T + T], v_sb[0:T, i % 3, c:c + DK], probT[0:T, b, par, h * T:h * T + T],
                                       start=True, stop=True)
                mm.then_inc(z_done, 1)

            def attention_out(t, between={}):
                r = rows_of[t]
                what = ("o", t)
                g_free(what)
                if t < last:
                    pe.wait_ge(z_made, 2 * (t + 2))
                for p in range(PAIRS):
                    if t == last and p % HB == 0:
                        pe.wait_ge(z_made, UNITS - 1 + p // HB)
                    mm = pe.matmul(g_bank(what)[0:r, 0:D], zT[:, p, P * t:P * t + r], wo_sb[:, p, :], start=(p == 0), stop=(p == PAIRS - 1))
                    for step in between.get(p, ()):
                        step()
                g_signal(what, mm)

            def flip_xn2(t):
                r = rows_of[t]
                what = ("t", t)
                g_free(what)
                pe.wait_ge(rec_made, t + 1)
                for k in range(KD):
                    mm = pe.transpose(g_bank(what)[:, k * r:k * r + r], rec[0:r, t, 0, k * P:(k + 1) * P], ident[0:r, 0:r])
                g_signal(what, mm)

            def router(t):
                r = rows_of[t]
                what = ("l", t)
                g_free(what)
                for k in range(KD):
                    mm = pe.matmul(g_bank(what)[0:r, 0:E], xn2T[:, k * r:k * r + r], wr_sb[:, k, :], start=(k == 0), stop=(k == KD - 1))
                g_signal(what, mm)

            def ranks(t):
                r = rows_of[t]
                what = ("r", t)
                g_free(what)
                dst = g_bank(what)[0:r, 0:E]
                pe.wait_ge(chosen_made, t + 1)
                pe.matmul(dst, before[0:r, 0:r], chosen[0:r, t, :], start=True, stop=False)
                g_signal(what, pe.matmul(dst, ones[:, 0:r], chosen_sum[:, t, :], start=False, stop=True))

            def dispatch(t):
                r = rows_of[t]
                pe.wait_ge(at_slot_made, t + 1)
                for k in range(KD):
                    mm = pe.matmul(bank[4 + k][:, 0:CAP], rec[0:r, t, 0, k * P:(k + 1) * P], at_slot[0:r, t, :],
                                   start=(t == 0), stop=(t == last))
                if t == last:
                    mm.then_inc(slotT_filled, 1)

            pe.wait_ge(wo_in, 16)
            pe.wait_ge(split_lo, 3)
            for i in (len(uses) - 8 + (7 - len(uses)) % 8,):
                s, v = emptied(i)
                pe.wait_ge(s, v)
            values(0)
            for name in ("q", "k"):
                s, v = emptied(number[name, (PAIRS - 1, 1)])
                pe.wait_ge(s, v)
            scores(0)
            values(1)
            for i in range(UNITS):
                if i + 1 < UNITS:
                    scores(i + 1)
                if i >= 6 and i % 2 == 0:
                    router((i - 6) // 2)
                if i >= 7 and i % 2:
                    ranks((i - 7) // 2)
                if i >= 1:
                    weigh(i - 1)
                if i + 2 < UNITS:
                    values(i + 2)
                flip(i)
                if i >= 5 and i % 2 and i + 1 < UNITS:
                    flip_xn2((i - 5) // 2)
                if i >= 4 and i % 2 == 0:
                    attention_out((i - 4) // 2)
            attention_out(last, {HB - 1: (lambda: weigh(UNITS - 1), lambda: flip_xn2(last - 1)),
                                 PAIRS - 3: (lambda: router(last - 1),)})
            pe.wait_ge(probT_made, 2 * UNITS)
            for t in range(last - 1):
                dispatch(t)
            ranks(last - 1)
            warm(9, Z)
            flip_xn2(last)
            warm(1, Z)
            router(last)
            dispatch(last - 1)
            warm(3, Z)
            ranks(last)
            warm(2, Z)
            dispatch(last)
            warm(2, Z)

            def flip_slots(e, b, n):
                pe.wait_ge(slots_in[b], 16 * n)
                for k in range(KD):
                    for s in range(2):
                        o = k * CAP + s * HALF
                        mm = pe.transpose(bank[7][:, o:o + HALF], slots[:, b, s, k * P:(k + 1) * P], ident[0:HALF, 0:HALF])
                mm.then_inc(slotT_filled, 1)

            def up(e, b, n, first_one=False):
                pe.wait_ge(w1_in[b], 16 * n)
                pe.wait_ge(slotT_made, e + 1)
                for m in range(MH):
                    j = m // 2
                    if m % 2 == 0 and not first_one:
                        pe.wait_ge(hid_made, MH // 2 * (e - 1) + j + 1)
                    for k in range(KD):
                        mm = pe.matmul(bank[j][:, (m % 2) * CAP:(m % 2) * CAP + CAP], w1_sb[:, b, k, m * P:(m + 1) * P], slotT[:, b, k, :],
                                       start=(k == 0), stop=(k == KD - 1))
                    if m % 2:
                        mm.then_inc(hid_filled, 1)

            def down(e, b, n, first_one=False, before_last=None):
                pe.wait_ge(w2_in[b], 16 * n)
                if not first_one:
                    pe.wait_ge(outT_made, e)
                for m in range(MH):
                    if m % 2 == 0:
                        pe.wait_ge(hid_made, MH // 2 * e + m // 2 + 1)
                    if m == MH - 1 and before_last:
                        before_last()
                    for d in range(KD):
                        mm = pe.matmul(bank[4 + d][:, 0:CAP], w2_sb[:, b, m, d * P:(d + 1) * P], hidT[:, b, m, :],
                                       start=(m == 0), stop=(m == MH - 1))
                mm.then_inc(out_filled, 1)

            def flip_out(e, b):
                pe.wait_ge(outT_made, e + 1)
                for s in range(2):
                    for d in range(KD):
                        o = s * D + d * P
                        mm = pe.transpose(bank[6][0:HALF, o:o + P], outT[:, b, d, s * HALF:(s + 1) * HALF], ident[:, :])
                mm.then_inc(y_filled, 1)

            def expert(e, b, n, n_next):
                up(e, b, n)
                pe.wait_ge(y_made, e - 1) if not isinstance(e, int) or e > 1 else None
                flip_out(e - 1, 1 - b)
                flip_slots(e + 1, 1 - b, n_next)
                down(e, b, n)

            pe.wait_ge(g_evac, len(g_uses))
            pe.wait_ge(last_evac, 4)
            up(0, 0, 1, first_one=True)
            down(0, 0, 1, first_one=True, before_last=lambda: flip_slots(1, 1, 1))
            expert(1, 1, 1, 1)
            with pe.Fori(2, E - 3, 2) as e:
                expert(e, 0, (e >> 1) + 1, (e >> 1) + 1)
                expert(e + 1, 1, (e >> 1) + 1, (e >> 1) + 1)
            expert(E - 2, 0, E // 2, E // 2)
            up(E - 1, 1, E // 2)
            pe.wait_ge(y_made, E - 2)
            flip_out(E - 2, 0)
            down(E - 1, 1, E // 2)
            pe.wait_ge(y_made, E - 1)
            flip_out(E - 1, 1)


_INS = ["x", "cls_tok", "L0_tok_W", "L0_tok_b", "L0_tok_cls_token", "L0_tok_pos_embed", "L0_attn_w_q", "L0_attn_w_k",
        "L0_attn_w_v", "L0_attn_w_o", "L0_ffn_Wr", "L0_ffn_br", "L0_ffn_W1", "L0_ffn_b1", "L0_ffn_W2", "L0_ffn_b2"]


def kernel(**inputs):
    import numpy as _np
    import concourse.bacc as _bacc
    from concourse import mybir as _mybir
    from concourse.bass_utils import run_bass_kernel_spmd as _run

    nc = _bacc.Bacc("TRN2", target_bir_lowering=False, num_devices=1)
    arrays, args = {}, []
    for name in _INS:
        a = _np.ascontiguousarray(inputs[name])
        arrays[f"in_{name}_dram"] = a
        args.append(nc.dram_tensor(f"in_{name}_dram", a.shape, _mybir.dt.from_np(a.dtype), kind="ExternalInput").ap())
    images = inputs["x"].shape[0]
    tokens = inputs["L0_tok_pos_embed"].shape[1] + 1
    experts = inputs["L0_ffn_W1"].shape[0]
    dim = inputs["cls_tok"].shape[2]
    n = images * tokens
    out = nc.dram_tensor("out_0_dram", (n + n * 2 // experts, dim), _mybir.dt.float32, kind="ExternalOutput").ap()
    vit_block(nc, *args, out)
    r = _run(nc, [arrays], core_ids=[0])
    return r.results[0]["out_0_dram"][:n].reshape(images, tokens, dim)
```

```python
from contextlib import ExitStack

import concourse.bass as bass
from concourse import mybir

ALU = mybir.AluOpType
ACT = mybir.ActivationFunctionType
AX = mybir.AxisListType
F32 = mybir.dt.float32
F32R = mybir.dt.float32r
BF16 = mybir.dt.bfloat16
I32 = mybir.dt.int32
U32 = mybir.dt.uint32

P = 128
EPS = 1e-5
MASKED = -1e30
SPLIT = ((0, 0), (0, 1), (1, 0))


def vit_block(nc, x, cls_tok, tok_w, tok_b, tok_cls, pos, wq, wk, wv, wo, wr, br, w1, b1, w2, b2, out):
    B, C, IMG, _ = x.shape
    D, PD = tok_w.shape
    S = pos.shape[1] + 1
    SIDE = int(round((PD // C) ** 0.5))
    NPH = IMG // SIDE
    H, _, DK = wq.shape
    E, _, HID = w1.shape
    N = B * S
    CAP = N * 2 // E
    HALF = CAP // 2
    KD = D // P
    KC = PD // P
    MH = HID // P
    PAIRS = H * DK // P
    TILES = -(-N // P)
    rows_of = [min(P, N - P * t) for t in range(TILES)]
    GB = P // S
    GT = GB * S
    GROUPS = -(-B // GB)
    tokens_of = [min(GT, N - GT * g) for g in range(GROUPS)]
    UNITS = 2 * GROUPS
    HU = H // 2
    HB = HU // 2
    NH = N // 2
    REC = D + 2
    TRASH = E * CAP
    assert KC == 2 * C and 2 * HALF == CAP and D == 2 * P and NPH * NPH + 2 == S and B * NPH <= P

    table = nc.dram_tensor("slot_table", [TRASH + 2 * N, REC], F32, kind="Internal").ap()

    with ExitStack() as ctx:
        def sb(name, shape, dt=F32):
            return ctx.enter_context(nc.sbuf_tensor(name, shape, dt))

        def sem(name):
            return ctx.enter_context(nc.semaphore(name))

        bank = [ctx.enter_context(nc.psum_tensor(f"bank{i}", [P, 512], F32)) for i in range(8)]

        xcols, imcols = KC * N, C * SIDE * IMG
        early = sb("early", [P, max(2 * PAIRS * N, imcols + xcols + KD * PD + KC * D)])
        images = early[0:B * NPH, 0:imcols].rearrange("p (c i w) -> p c i w", c=C, i=SIDE)
        patchT = early[:, imcols:imcols + xcols].rearrange("p (k n) -> p k n", k=KC)
        at = imcols + xcols
        w_in = early[:, at:at + KD * PD].rearrange("p (k n) -> p k n", k=KD)
        at += KD * PD
        w_inT = early[:, at:at + KC * D].rearrange("p (k n) -> p k n", k=KC)
        qT = early[:, 0:PAIRS * N].rearrange("p (h n) -> p h n", h=PAIRS)
        kT = early[:, PAIRS * N:2 * PAIRS * N].rearrange("p (h n) -> p h n", h=PAIRS)
        at = 2 * MH * CAP
        hidT = early[:, 0:at].rearrange("p (b m n) -> p b m n", b=2, m=MH)
        slotT = early[:, at:at + 2 * KD * CAP].rearrange("p (b k n) -> p b k n", b=2, k=KD)
        at += 2 * KD * CAP
        outT = early[:, at:at + 2 * KD * CAP].rearrange("p (b k n) -> p b k n", b=2, k=KD)
        at += 2 * KD * CAP
        y_sb = early[0:HALF, at:at + 4 * D].rearrange("p (b s d) -> p b s d", b=2, s=2)

        at = 2 * PAIRS * N
        at_slot = early[:, at:at + TILES * CAP].rearrange("p (t c) -> p t c", t=TILES)
        at += TILES * CAP
        slot_no = early[:, at:at + CAP]

        with ExitStack() as stage2:
            def split(name, scope=stage2):
                return [scope.enter_context(nc.sbuf_tensor(f"{name}_{part}", [P, KD, H * DK], F32R)) for part in ("hi", "lo")]

            wq_r, wk_r = split("wq"), split("wk")
        v_sb = sb("v_sb", [P, 3, HU * DK])
        prob = sb("prob", [P, 2, 2, HB * GT])
        probT = sb("probT", [P, 2, 2, HB * GT])
        xn2T = sb("xn2T", [P, KD * P])
        zT_lo = sb("zT_lo", [P, 2, PAIRS, P], F32R)
        left = 4 * KD * H * DK - (3 * HU * DK + 8 * HB * GT + KD * P + 2 * PAIRS * P)
        assert left >= 0
        sb("unused", [P, left])
        wv_r = split("wv", ctx)
        wo_r = [sb(f"wo_{part}", [P, PAIRS, D], F32R) for part in ("hi", "lo")]
        wr_sb = sb("wr_sb", [P, KD, E])
        br_sb = sb("br_sb", [P, E])
        rows = sb("rows", [P, 2 * TILES * D + 2 * TILES * REC])
        h_sb, xn_sb = (rows[:, a:a + TILES * D].rearrange("p (t d) -> p t d", t=TILES)
                       for a in (0, TILES * D))
        rec = rows[:, 2 * TILES * D:2 * TILES * D + 2 * TILES * REC].rearrange("p (t k c) -> p t k c", t=TILES, k=2)
        patches = rows[0:B * NPH, 0:imcols].rearrange("p (c w n) -> p c w n", c=C, w=NPH)
        xnT = [sb(f"xnT_{part}", [P, KD, N], F32R) for part in ("hi", "lo")]
        zT = sb("zT", [P, PAIRS, N], F32R)
        w1_sb = sb("w1_sb", [P, 2, KD, HID])
        w2_sb = sb("w2_sb", [P, 2, MH, D])
        raw = [w.rearrange("p a b -> p (a b)").rearrange("p (h k n) -> p h k n", h=H, k=KD)
               for w in (w1_sb[:, 0], w1_sb[:, 1], w2_sb[:, 0])]
        raw_wo = w2_sb[:, 1]
        raw_by_chunk = [w.rearrange("p h k n -> p k h n") for w in raw]
        assert HID == H * DK and PAIRS == MH
        bias_rows = sb("bias_rows", [P, P])
        biasT = sb("biasT", [P, E * (MH + KD)])
        slots = sb("slots", [HALF, 2, 2, REC])
        slot_meta = sb("slot_meta", [HALF, E, 2, 2])
        token = sb("token", [HALF, 2, 2], U32)
        ident = sb("ident", [P, P])
        spread = sb("spread", [P // 2 + S, B, S], F32R)
        base = sb("base", [S, D])
        base_add = sb("base_add", [S, D])
        base_r = sb("base_r", [P // 2 + S, D], F32R)
        own = sb("own", [P, GT], BF16)
        other = sb("other", [P, HB * GT], BF16)
        before = sb("before", [P, P], BF16)
        ones = sb("ones", [P, P], BF16)
        eps = sb("eps", [P, 1])
        expert_no = sb("expert_no", [P, E])
        trash_row = sb("trash_row", [P, TILES, 2])
        slot_base = sb("slot_base", [P, TILES, 2, E])
        blank = sb("blank", [HALF, 2, REC])
        stats = sb("stats", [P, 2, 6])
        mv = sb("mv", [P, 2 * TILES, 2])
        lnv = sb("lnv", [P, 2 * TILES])
        rstd0 = sb("rstd0", [P, 2 * TILES])
        newton = sb("newton", [P, 2, TILES])
        rstd = sb("rstd", [P, 2 * TILES])
        negmax = sb("negmax", [P, UNITS, HU])
        den = sb("den", [P, UNITS, HU])
        rden = sb("rden", [P, UNITS, HU])
        first_takes = sb("first_takes", [P, TILES])
        logits = sb("logits", [P, E])
        top = sb("top", [P, 8])
        topi = sb("topi", [P, 8], U32)
        topf = sb("topf", [P, 2])
        hot = sb("hot", [P, TILES, 2, E])
        chosen = sb("chosen", [P, TILES, E], BF16)
        chosen_sum = sb("chosen_sum", [P, TILES, E], BF16)
        gap = sb("gap", [P, TILES])
        egap = sb("egap", [P, TILES])
        gsum = sb("gsum", [P, TILES])
        where = sb("where", [P, 2, E])
        kept = sb("kept", [P, TILES, 2, E])
        picked = sb("picked", [P, 2, E])
        row = sb("row", [P, 2])
        row_no = sb("row_no", [P, TILES, 2], U32)

        x_in = [sem(f"x_in{c}") for c in range(C)]
        w_in_in = [sem(f"w_in_in{c}") for c in range(C)]
        wq_in, wk_in, wv_in, wo_in = (sem(n) for n in ("wq_in", "wk_in", "wv_in", "wo_in"))
        split_hi, split_lo = sem("split_hi"), sem("split_lo")
        z_hi_made = sem("z_hi_made")
        xnT_hi_made = sem("xnT_hi_made")
        small_in = sem("small_in")
        base_in = sem("base_in")
        w1_in = [sem(f"w1_in{i}") for i in range(2)]
        w2_in = [sem(f"w2_in{i}") for i in range(2)]
        meta_in = sem("meta_in")
        slots_in = [sem(f"slots_in{i}") for i in range(2)]
        zeroed, ident_made, patch_zeroed, const_made = (sem(n) for n in ("zeroed", "ident_made", "patch_zeroed", "const_made"))
        zeroed_dve = sem("zeroed_dve")
        base_made = sem("base_made")
        sorted_act, sorted_dve = sem("sorted_act"), sem("sorted_dve")
        filled = sem("filled")
        evac_dve, evac_act = sem("evac_dve"), sem("evac_act")
        dve_chain = sem("dve_chain")
        pool_chain = sem("pool_chain")
        act_chain = sem("act_chain")
        var_made, rstd_made = sem("var_made"), sem("rstd_made")
        xn_made, hx_made = sem("xn_made"), sem("hx_made")
        scored, maxed, exped, rden_made, prob_made = (sem(n) for n in ("scored", "maxed", "exped", "rden_made", "prob_made"))
        flipped, probT_made, z_done, z_made = (sem(n) for n in ("flipped", "probT_made", "z_done", "z_made"))
        last_filled, last_evac = sem("last_filled"), sem("last_evac")
        g_filled, g_evac = sem("g_filled"), sem("g_evac")
        rec_made, rec_copied, gap_made, gsum_made, chosen_made = (
            sem(n) for n in ("rec_made", "rec_copied", "gap_made", "gsum_made", "chosen_made"))
        at_slot_made, slot_no_made = sem("at_slot_made"), sem("slot_no_made")
        first_gate_made = sem("first_gate_made")
        blanked = sem("blanked")
        outT_half_made, y_half_filled, y_half_made = sem("outT_half_made"), sem("y_half_filled"), sem("y_half_made")
        scattered = sem("scattered")
        h2_out = sem("h2_out")
        slotT_filled, slotT_made = sem("slotT_filled"), sem("slotT_made")
        hid_filled, hid_made, out_filled, outT_made = (sem(n) for n in ("hid_filled", "hid_made", "out_filled", "outT_made"))
        y_filled, y_made, added = sem("y_filled"), sem("y_made"), sem("added")

        shared = range(TILES, 8)
        uses = []

        def use(what, eng, banks):
            uses.append((what, eng, banks[sum(u[2] in banks for u in uses) % len(banks)]))

        for c in range(C):
            for k in (2 * c, 2 * c + 1):
                use(("x", (k, 0)), "act", shared)
                use(("x", (k, 1)), "dve", shared)
            use(("w", c), "act", shared)
        HT = (NH - 1) // P + 1
        assert HT == TILES - 2
        for t in range(TILES):
            use(("h", t), "act", [t])
        for t in range(HT):
            use(("xn", t), "dve", shared)
        use(("bias", 0), "dve", shared)
        for half in range(2):
            for p in range(PAIRS):
                use(("q", (p, half)), "act", range(8))
                use(("k", (p, half)), "dve", range(8))
                if half == 0 and p in (1, 2):
                    use(("xn", HT + p - 1), "dve", range(8))
        number = {what: i for i, (what, _, _) in enumerate(uses)}
        bank_of = [bank[b] for _, _, b in uses]

        def emptied(i):
            eng = uses[i][1]
            return (evac_dve if eng == "dve" else evac_act), sum(u[1] == eng for u in uses[:i + 1])

        def use_before(b, i):
            return max((j for j in range(i) if uses[j][2] == b), default=None)

        g_uses = [("v", 0), ("v", 1)]
        for i in range(UNITS):
            if i >= 6 and i % 2 == 0:
                g_uses.append(("l", (i - 6) // 2))
            if i >= 7 and i % 2:
                g_uses.append(("r", (i - 7) // 2))
            if i + 2 < UNITS:
                g_uses.append(("v", i + 2))
            if i >= 5 and i % 2 and i + 1 < UNITS:
                g_uses.append(("t", (i - 5) // 2))
            if i >= 4 and i % 2 == 0:
                g_uses.append(("o", (i - 4) // 2))
        last = TILES - 1
        assert UNITS == 2 * last + 4
        g_uses += [("t", last - 1), ("l", last - 1), ("r", last - 1)]
        g_number = {u: i for i, u in enumerate(g_uses)}
        assert len(g_number) == len(g_uses)
        last_bank = {"o": bank[0], "t": bank[1], "l": bank[2], "r": bank[3]}
        G = bank[7]
        Z = bank[6]

        def g_bank(what):
            return G if what in g_number else last_bank[what[0]]

        def span(i):
            return GT * (i // 2), tokens_of[i // 2], i % 2

        def patch_cols(dst, k, part):
            v = dst[:, k, :].rearrange("p (b s) -> p b s", s=S)[:, :, 2:S]
            return v.rearrange("p b (f w) -> p w b f", w=NPH)[:, 3 * part:3 * part + 3]

        def pixels(c, part):
            src = images[:, c].rearrange("p i (w j) -> p w i j", j=SIDE)[:, 3 * part:3 * part + 3]
            return patches[:, c, 3 * part:3 * part + 3, :].rearrange("p w (i j) -> p w i j", i=SIDE), src

        def load_w_in(eng, c):
            cols = slice(2 * c * P, (2 * c + 2) * P)
            eng.dma_start(w_in[:, :, cols], tok_w[:, cols].rearrange("(k p) n -> p k n", p=P)).then_inc(w_in_in[c], 16)

        block = ctx.enter_context(nc.Block())

        @block.sync
        def _(sp):
            for c in range(C):
                sp.dma_start(images[:, c], x[:, c].rearrange("b (f i) w -> b f (i w)", i=SIDE)).then_inc(x_in[c], 16)
                if c:
                    load_w_in(sp, c)
            sp.dma_start(base[1:S, :], pos[0]).then_inc(base_in, 16)
            sp.dma_start(base[0:1, :], cls_tok[0]).then_inc(base_in, 16)
            sp.dma_start(base_add[1:2, :], tok_cls[0]).then_inc(base_in, 16)
            sp.dma_start(base_add[2:S, :], tok_b.rearrange("(a d) -> a d", a=1).to_broadcast([S - 2, D])).then_inc(base_in, 16)
            for w, dst, done in ((wq, raw[0], wq_in), (wk, raw[1], wk_in), (wv, raw[2], wv_in)):
                sp.dma_start(dst, w.rearrange("h (p k) n -> p h k n", k=KD)).then_inc(done, 16)
            sp.dma_start(bias_rows[0:E * MH, :], b1.rearrange("e (m p) -> (e m) p", p=P)).then_inc(small_in, 16)
            sp.dma_start(bias_rows[E * MH:E * (MH + KD), :], b2.rearrange("e (m p) -> (e m) p", p=P)).then_inc(small_in, 16)
            sp.dma_start(wr_sb[:, :, :], wr.rearrange("(k p) e -> p k e", p=P)).then_inc(small_in, 16)
            sp.dma_start(br_sb[:, :], br.rearrange("(a e) -> a e", a=1).to_broadcast([P, E])).then_inc(small_in, 16)
            sp.dma_start(raw_wo, wo.rearrange("(t p) d -> p t d", p=P)).then_inc(wo_in, 16)
            sp.wait_ge(const_made, 1)
            for s in range(2):
                sp.dma_start(table[0:TRASH, :].rearrange("(e s p) c -> s p e c", p=HALF, s=2)[s],
                             blank[:, s:s + 1, :].to_broadcast([HALF, E, REC])).then_inc(blanked, 16)
            sp.dma_start(out[N:N + CAP, :].rearrange("(s p) d -> p s d", p=HALF), blank[:, :, 0:D]).then_inc(h2_out, 16)
            sp.wait_ge(split_lo, 4)
            for e in range(2):
                sp.dma_start(w1_sb[:, e], w1[e].rearrange("(k p) n -> p k n", p=P)).then_inc(w1_in[e], 16)
                sp.dma_start(w2_sb[:, e], w2[e].rearrange("(m p) n -> p m n", p=P)).then_inc(w2_in[e], 16)
            for t in range(TILES):
                sp.wait_ge(var_made, TILES + t + 1)
                sp.dma_start(out[P * t:P * t + rows_of[t], :], h_sb[0:rows_of[t], t, :]).then_inc(h2_out, 16)

            def load_slots(e, b):
                src = table[bass.ds(e * CAP, CAP), :].rearrange("(s p) c -> p s c", p=HALF)
                sp.dma_start(slots[:, b], src).then_inc(slots_in[b], 16)

            sp.wait_ge(scattered, 16 * 2 * TILES)
            load_slots(1, 1)
            sp.dma_start(slot_meta[:, :, :, :], table[0:TRASH, D:REC].rearrange("(e s p) c -> p e s c", p=HALF, s=2)).then_inc(meta_in, 16)

            def refill(e, b):
                sp.wait_ge(slotT_filled, e + 1)
                load_slots(e + 2, b)
                sp.wait_ge(hid_filled, MH // 2 * (e + 1))
                sp.dma_start(w1_sb[:, b], w1[bass.ds(e + 2, 1)].rearrange("a (k p) n -> p (a k) n", p=P)).then_inc(w1_in[b], 16)
                sp.wait_ge(out_filled, e + 1)
                sp.dma_start(w2_sb[:, b], w2[bass.ds(e + 2, 1)].rearrange("a (m p) n -> p (a m) n", p=P)).then_inc(w2_in[b], 16)

            with sp.Fori(0, E - 3, 2) as e:
                refill(e, 0)
                refill(e + 1, 1)
            sp.wait_ge(h2_out, 16 * (TILES + 1))
            sp.wait_ge(added, 32 * E)

        @block.gpsimd
        def _(pool):
            count = [0]

            def chained(ins):
                count[0] += 1
                ins.then_inc(pool_chain, 1)
                pool.wait_ge(pool_chain, count[0])

            nc.gpsimd.memset(ident[:, :], 0.0).then_inc(zeroed, 1)
            pool.wait_ge(zeroed, 1)
            nc.gpsimd.affine_select(out=ident[:, :], in_=ident[:, :], compare_op=ALU.not_equal, fill=1.0, base=0,
                                    pattern=[[1, P]], channel_multiplier=-1).then_inc(ident_made, 1)
            nc.gpsimd.memset(patchT[:, :, :].rearrange("p k (b s) -> p (k b) s", s=S)[:, :, 0:2], 0.0).then_inc(patch_zeroed, 1)
            chained(nc.gpsimd.memset(spread[:, :, :].bitcast(F32), 0.0))
            for lo in (0, P // 2):
                part = spread[lo:lo + S, :, :]
                chained(nc.gpsimd.affine_select(out=part, in_=part, compare_op=ALU.not_equal, fill=1.0,
                                                base=0, pattern=[[0, B], [1, S]], channel_multiplier=-1))
            nc.gpsimd.memset(eps[:, :], EPS)
            for lo in (0, P // 2):
                o3 = own[lo:lo + GB, :].rearrange("p (a s) -> p a s", s=S)
                m3 = other[lo:lo + GB, :].rearrange("p (h a s) -> p h a s", a=GB, s=S)
                chained(nc.gpsimd.memset(o3, 0.0))
                chained(nc.gpsimd.affine_select(out=o3, in_=o3, compare_op=ALU.not_equal, fill=1.0, base=0,
                                                pattern=[[1, GB], [0, S]], channel_multiplier=-1))
                chained(nc.gpsimd.memset(m3, MASKED))
                chained(nc.gpsimd.affine_select(out=m3, in_=m3, compare_op=ALU.not_equal, fill=0.0, base=0,
                                                pattern=[[0, HB], [1, GB], [0, S]], channel_multiplier=-1))
            chained(nc.gpsimd.memset(ones[:, :], 1.0))
            chained(nc.gpsimd.affine_select(out=before[:, :], in_=ones[:, :], compare_op=ALU.is_ge, fill=0.0, base=-1,
                                            pattern=[[1, P]], channel_multiplier=-1))
            nc.gpsimd.iota(expert_no[:, :], pattern=[[1, E]], base=0, channel_multiplier=0,
                           allow_small_or_imprecise_dtypes=True)
            nc.gpsimd.iota(slot_base[:, :, :, :], pattern=[[-P, TILES], [-N, 2], [CAP, E]], base=-TRASH, channel_multiplier=-1,
                           allow_small_or_imprecise_dtypes=True)
            nc.gpsimd.iota(trash_row[:, :, :], pattern=[[P, TILES], [N, 2]], base=TRASH, channel_multiplier=1,
                           allow_small_or_imprecise_dtypes=True)
            chained(nc.gpsimd.memset(blank[:, :, :], 0.0))
            chained(nc.gpsimd.iota(blank[:, :, D].bitcast(I32), pattern=[[HALF, 2]], base=N, channel_multiplier=1))
            nc.gpsimd.memset(chosen_sum[:, 0, :], 0.0).then_inc(const_made, 1)

            def residual(t):
                r = rows_of[t]
                pool.wait_ge(xn_made, t + 1)
                nc.gpsimd.tensor_tensor(h_sb[0:r, t, :], h_sb[0:r, t, :], xn_sb[0:r, t, :], ALU.add).then_inc(hx_made, 1)

            def round_rest(n):
                pool.wait_ge(split_hi, n + 1)
                lo, hi = (part[:, :, :].rearrange("p k (h n) -> p k h n", h=H) for part in (wq_r, wk_r, wv_r)[n][::-1])
                nc.gpsimd.tensor_tensor(lo, raw_by_chunk[n], hi.bitcast(F32), ALU.subtract).then_inc(split_lo, 1)

            round_rest(0)
            round_rest(1)
            for t in range(TILES):
                residual(t)
            chained(nc.gpsimd.iota(rec[:, :, :, D].bitcast(I32), pattern=[[P, TILES], [0, 2]], base=0, channel_multiplier=1))
            nc.gpsimd.iota(slot_no, pattern=[[1, CAP]], base=0, channel_multiplier=0,
                           allow_small_or_imprecise_dtypes=True).then_inc(slot_no_made, 1)
            round_rest(2)
            pool.wait_ge(split_hi, 4)
            nc.gpsimd.tensor_tensor(wo_r[1][:, :, :], raw_wo, wo_r[0][:, :, :].bitcast(F32), ALU.subtract).then_inc(split_lo, 1)

            def normalise(i):
                _, T, b = span(i)
                for par in range(2):
                    pool.wait_ge(rden_made, 2 * i + par + 1)
                    v = prob[0:T, b, par, 0:HB * T].rearrange("p (h m) -> p h m", h=HB)
                    r = rden[0:T, i, HB * par:HB * par + HB].rearrange("p (h a) -> p h a", a=1).to_broadcast([T, HB, T])
                    nc.gpsimd.tensor_tensor(v, v, r, ALU.mult).then_inc(prob_made, 1)

            def second_gate(t):
                r = rows_of[t]
                pool.wait_ge(first_gate_made, t + 1)
                chained(nc.gpsimd.tensor_tensor(rec[0:r, t, 1, D + 1:D + 2], rec[0:r, t, 0, D + 1:D + 2], egap[0:r, t:t + 1],
                                                ALU.mult))

            def rows_out(t):
                r = rows_of[t]
                if t < last:
                    pool.wait_ge(g_evac, g_number["r", t] + 1)
                else:
                    pool.wait_ge(last_evac, len(last_bank))
                chained(nc.gpsimd.tensor_tensor(picked[0:r, :, :], hot[0:r, t, :, :], kept[0:r, t, :, :], ALU.mult))
                w = E
                while w > 1:
                    w //= 2
                    chained(nc.gpsimd.tensor_tensor(picked[0:r, :, 0:w], picked[0:r, :, 0:w], picked[0:r, :, w:2 * w], ALU.add))
                chained(nc.gpsimd.tensor_tensor(row[0:r, :], picked[0:r, :, 0], trash_row[0:r, t, :], ALU.add))
                chained(nc.gpsimd.tensor_copy(row_no[0:r, t, :], row[0:r, :]))

            def scatter(t):
                r = rows_of[t]
                rows_out(t)
                second_gate(t)
                if t == 0:
                    pool.wait_ge(blanked, 32)
                pool.wait_ge(rec_copied, t + 1)
                for k in range(2):
                    pool.indirect_dma_start(
                        table, bass.IndirectOffsetOnAxis(ap=row_no[0:r, t, k:k + 1], axis=0),
                        rec[0:r, t, k, :], None).then_inc(scattered, 16)

            for i in range(UNITS):
                normalise(i)
                if i == UNITS - 3:
                    scatter(0)
            for t in range(1, TILES):
                scatter(t)

            pool.wait_ge(h2_out, 16 * (TILES + 1))
            for e in range(E):
                pool.wait_ge(y_made, e + 1)
                if e:
                    pool.wait_ge(added, 32 * e)
                for s in range(2):
                    if (e, s) == (E - 1, 1):
                        pool.wait_ge(y_half_made, 1)
                    pool.indirect_dma_start(
                        out, bass.IndirectOffsetOnAxis(ap=token[:, e % 2, s:s + 1], axis=0),
                        y_sb[:, e % 2, s, :], None, compute_op=ALU.add).then_inc(added, 16)

        @block.scalar
        def _(act):
            load_w_in(act, 0)
            nc.scalar.preload_act_table_set("natural_log_exp_and_others")

            count = [0]

            def chained(ins):
                count[0] += 1
                ins.then_inc(act_chain, 1)
                act.wait_ge(act_chain, count[0])

            def patches_out(k, part):
                i = number["x", (k, part)]
                act.wait_ge(filled, i + 1)
                src = bank_of[i][:, 0:3 * B * NPH].rearrange("p (w b f) -> p w b f", w=3, b=B)
                nc.scalar.copy(patch_cols(patchT, k, part), src).then_inc(evac_act, 1)

            def sort(c):
                act.wait_ge(x_in[c], 16)
                nc.scalar.copy(*pixels(c, 0)).then_inc(sorted_act, 1)

            def round_weights(n):
                act.wait_ge((wq_in, wk_in, wv_in)[n], 16)
                hi = (wq_r, wk_r, wv_r)[n][0][:, :, :].rearrange("p k (h n) -> p k h n", h=H)
                nc.scalar.copy(hi, raw_by_chunk[n]).then_inc(split_hi, 1)

            sort(0)
            act.wait_ge(patch_zeroed, 1)
            for c in range(C):
                patches_out(2 * c, 0)
                patches_out(2 * c + 1, 0)
                i = number["w", c]
                act.wait_ge(filled, i + 1)
                nc.scalar.copy(w_inT[:, 2 * c:2 * c + 2, :], bank_of[i][:, 0:2 * D].rearrange("p (k n) -> p k n", k=2)).then_inc(evac_act, 1)
                if c + 1 < C:
                    sort(c + 1)
                if c == C - 2:
                    round_weights(0)

            def rstd_guess(j, r, n=1):
                act.wait_ge(var_made, j + n)
                chained(nc.scalar.activation(lnv[0:r, j:j + n], mv[0:r, j:j + n, 1], ACT.Ln, bias=eps[0:r, :]))
                nc.scalar.activation(rstd0[0:r, j:j + n], lnv[0:r, j:j + n], ACT.Exp, scale=-0.5).then_inc(rstd_made, n)

            def h_out(t):
                i = number["h", t]
                r = rows_of[t]
                act.wait_ge(filled, i + 1)
                nc.scalar.copy(h_sb[0:r, t, :], bank_of[i][0:r, 0:D]).then_inc(evac_act, 1)

            def xnT_hi_out(t):
                i, r = number["xn", t], rows_of[t]
                act.wait_ge(filled, i + 1)
                nc.scalar.copy(xnT[0][:, :, P * t:P * t + r], bank_of[i][:, 0:KD * r].rearrange("p (k n) -> p k n", k=KD)).then_inc(xnT_hi_made, 1)

            round_weights(1)
            act.wait_ge(const_made, 1)
            for t in range(HT):
                h_out(t)
            rstd_guess(0, P, HT)
            h_out(HT)
            for t in range(HT):
                xnT_hi_out(t)
            rstd_guess(HT, P)
            h_out(HT + 1)
            rstd_guess(HT + 1, rows_of[HT + 1])
            for half in range(2):
                for p in range(PAIRS):
                    i = number["q", (p, half)]
                    act.wait_ge(filled, i + 1)
                    nc.scalar.mul(qT[:, p, NH * half:NH * half + NH], bank_of[i][:, 0:NH], float(DK) ** -0.5).then_inc(evac_act, 1)
                    if half == 0 and p in (1, 2):
                        xnT_hi_out(HT + p - 1)
                    if (half, p) == (0, 4):
                        round_weights(2)
                    if (half, p) == (0, 6):
                        act.wait_ge(wo_in, 16)
                        nc.scalar.copy(wo_r[0][:, :, :], raw_wo).then_inc(split_hi, 1)

            def exponentials(i, par):
                _, T, b = span(i)
                act.wait_ge(maxed, 2 * i + par + 1)
                if i >= 2:
                    act.wait_ge(flipped, 2 * (i - 2) + par + 1)
                for h in range(HB):
                    j = HB * par + h
                    ins = nc.scalar.activation(prob[0:T, b, par, h * T:h * T + T], bank[2 * b + par][0:T, h * T:h * T + T],
                                               ACT.Exp, bias=negmax[0:T, i, j:j + 1], accum_out=den[0:T, i, j:j + 1])
                ins.then_inc(exped, 1)

            def v_out(i):
                _, T, _ = span(i)
                act.wait_ge(g_filled, g_number["v", i] + 1)
                if i >= 3:
                    act.wait_ge(z_done, i - 2)
                nc.scalar.copy(v_sb[0:T, i % 3, :], G[0:T, :]).then_inc(g_evac, 1)

            def z_first(i):
                return i % 2 == 0 or i == UNITS - 1

            def z_out(i):
                o, T, _ = span(i)
                act.wait_ge(z_done, i + 1)
                nc.scalar.copy(zT[:, HB * (i % 2):HB * (i % 2) + HB, o:o + T],
                               Z[:, 0:HB * T].rearrange("p (h n) -> p h n", h=HB)).then_inc(z_hi_made, 1)

            def gate_exp(t):
                r = rows_of[t]
                act.wait_ge(gap_made, t + 1)
                chained(nc.scalar.activation(egap[0:r, t:t + 1], gap[0:r, t:t + 1], ACT.Exp))
                nc.scalar.activation(gsum[0:r, t:t + 1], egap[0:r, t:t + 1], ACT.Copy, bias=1.0).then_inc(gsum_made, 1)

            def second_record(t):
                r = rows_of[t]
                act.wait_ge(rec_made, t + 1)
                nc.scalar.copy(rec[0:r, t, 1, 0:D], rec[0:r, t, 0, 0:D]).then_inc(rec_copied, 1)

            exponentials(0, 0)
            v_out(1)
            exponentials(0, 1)
            for i in range(UNITS):
                if i >= 1 and z_first(i):
                    z_out(i - 1)
                if i >= 5 and i % 2:
                    rstd_guess(TILES + (i - 5) // 2, rows_of[(i - 5) // 2])
                if i + 1 < UNITS:
                    exponentials(i + 1, 0)
                if i >= 1 and not z_first(i):
                    z_out(i - 1)
                if i + 2 < UNITS and i % 2:
                    v_out(i + 2)
                if i + 1 < UNITS:
                    exponentials(i + 1, 1)
                if i >= 7 and i % 2:
                    gate_exp((i - 7) // 2)
                if i >= 5 and i % 2 and i + 1 < UNITS:
                    second_record((i - 5) // 2)
            z_out(UNITS - 1)
            second_record(last - 1)
            gate_exp(last - 1)
            rstd_guess(TILES + last, rows_of[last])
            second_record(last)
            gate_exp(last)

            def gelu(e, b):
                for j in range(MH // 2):
                    act.wait_ge(hid_filled, MH // 2 * e + j + 1)
                    for m in (2 * j, 2 * j + 1):
                        bias = biasT[:, bass.ds(e * MH + m, 1)]
                        ins = nc.scalar.activation(hidT[:, b, m, :], bank[j][:, (m % 2) * CAP:(m % 2) * CAP + CAP], ACT.Gelu, bias=bias)
                    ins.then_inc(hid_made, 1)

            nc.scalar.preload_act_table(ACT.Gelu)
            act.wait_ge(slotT_filled, 1)
            for k in range(KD):
                ins = nc.scalar.copy(slotT[:, 0, k, :], bank[4 + k][:, 0:CAP])
            ins.then_inc(slotT_made, 1)
            gelu(0, 0)
            gelu(1, 1)
            with act.Fori(2, E - 1, 2) as e:
                act.wait_ge(out_filled, e - 1)
                gelu(e, 0)
                act.wait_ge(out_filled, e)
                gelu(e + 1, 1)
            act.wait_ge(out_filled, E)
            e, d = E - 1, KD - 1
            nc.scalar.activation(outT[:, 1, d, :], bank[4 + d][:, 0:CAP], ACT.Identity,
                                 bias=biasT[:, E * MH + e * KD + d:E * MH + e * KD + d + 1]).then_inc(outT_half_made, 1)
            act.wait_ge(y_half_filled, 1)
            act.wait_ge(added, 32 * (E - 2))
            nc.scalar.mul(y_sb[:, 1, 1, :], bank[7][0:HALF, 0:D], slot_meta[:, e, 1, 1:2]).then_inc(y_half_made, 1)

        @block.vector
        def _(dve):
            count = [0]

            def chained(ins):
                count[0] += 1
                ins.then_inc(dve_chain, 1)
                dve.wait_ge(dve_chain, count[0])

            chained(nc.vector.memset(base_add[0:1, :], 0.0))
            chained(nc.vector.memset(base_r[:, :].bitcast(F32), 0.0))

            def sort(c):
                dve.wait_ge(x_in[c], 16)
                nc.vector.tensor_copy(*pixels(c, 1)).then_inc(sorted_dve, 1)

            sort(0)
            dve.wait_ge(patch_zeroed, 1)
            for c in range(C):
                for k in (2 * c, 2 * c + 1):
                    i = number["x", (k, 1)]
                    dve.wait_ge(filled, i + 1)
                    src = bank_of[i][:, 0:3 * B * NPH].rearrange("p (w b f) -> p w b f", w=3, b=B)
                    nc.vector.tensor_copy(patch_cols(patchT, k, 1), src).then_inc(evac_dve, 1)
                if c + 1 < C:
                    sort(c + 1)
                if c == C - 2:
                    dve.wait_ge(base_in, 64)
                    chained(nc.vector.tensor_tensor(base[:, :], base[:, :], base_add[:, :], ALU.add))
                    chained(nc.vector.tensor_copy(base_r[0:S, :], base[:, :]))
                    nc.vector.tensor_tensor(base_r[P // 2:P // 2 + S, :], base[:, :], base_r[0:S, :].bitcast(F32),
                                            ALU.subtract).then_inc(base_made, 1)

            def variance(src, j, r):
                chained(nc.vector.bn_stats(stats[0:r, j % 2, :], src))
                nc.vector.bn_aggr(mv[0:r, j, :], stats[0:r, j % 2, :]).then_inc(var_made, 1)

            def newton_step(j, r, n=1):
                dve.wait_ge(rstd_made, j + n)
                a, b = newton[0:r, 0, 0:n], newton[0:r, 1, 0:n]
                chained(nc.vector.tensor_tensor(a, rstd0[0:r, j:j + n], rstd0[0:r, j:j + n], ALU.mult))
                chained(nc.vector.scalar_tensor_tensor(out=b, in0=mv[0:r, j:j + n, 1], scalar=EPS, in1=a, op0=ALU.add, op1=ALU.mult))
                chained(nc.vector.tensor_scalar(a, b, -0.5, 1.5, ALU.mult, ALU.add))
                chained(nc.vector.tensor_tensor(rstd[0:r, j:j + n], a, rstd0[0:r, j:j + n], ALU.mult))

            def layernorm(dst, src, j, r):
                return nc.vector.tensor_scalar(dst, src, mv[0:r, j, 0:1], rstd[0:r, j:j + 1], ALU.subtract, ALU.mult)

            def xnT_lo_out(t):
                i, r = number["xn", t], rows_of[t]
                dve.wait_ge(xnT_hi_made, t + 1)
                src = bank_of[i][:, 0:KD * r].rearrange("p (k n) -> p k n", k=KD)
                nc.vector.tensor_tensor(xnT[1][:, :, P * t:P * t + r], src, xnT[0][:, :, P * t:P * t + r].bitcast(F32),
                                        ALU.subtract).then_inc(evac_dve, 1)

            def first_variance(t):
                s, v = emptied(number["h", t])
                dve.wait_ge(s, v)
                variance(h_sb[0:rows_of[t], t, :], t, rows_of[t])

            def first_layernorm(t):
                r = rows_of[t]
                layernorm(xn_sb[0:r, t, :], h_sb[0:r, t, :], t, r).then_inc(xn_made, 1)

            for t in range(HT):
                first_variance(t)
            newton_step(0, P, HT)
            for t in range(HT):
                first_layernorm(t)
            first_variance(HT)
            for t in range(HT):
                xnT_lo_out(t)
            newton_step(HT, P)
            first_layernorm(HT)
            first_variance(HT + 1)
            newton_step(HT + 1, rows_of[HT + 1])
            first_layernorm(HT + 1)
            i = number["bias", 0]
            dve.wait_ge(filled, i + 1)
            nc.vector.tensor_copy(biasT[:, :], bank_of[i][:, 0:E * (MH + KD)]).then_inc(evac_dve, 1)
            for half in range(2):
                for p in range(PAIRS):
                    i = number["k", (p, half)]
                    dve.wait_ge(filled, i + 1)
                    nc.vector.tensor_copy(kT[:, p, NH * half:NH * half + NH], bank_of[i][:, 0:NH]).then_inc(evac_dve, 1)
                    if half == 0 and p in (1, 2):
                        xnT_lo_out(HT + p - 1)

            def row_max(i):
                _, T, b = span(i)
                for par in range(2):
                    dve.wait_ge(scored, 2 * i + par + 1)
                    nc.vector.tensor_reduce(negmax[0:T, i, HB * par:HB * par + HB],
                                            bank[2 * b + par][0:T, 0:HB * T].rearrange("p (h m) -> p h m", h=HB),
                                            AX.X, ALU.max, negate=True).then_inc(maxed, 1)

            def row_rden(i):
                _, T, _ = span(i)
                for par in range(2):
                    dve.wait_ge(exped, 2 * i + par + 1)
                    nc.vector.reciprocal(rden[0:T, i, HB * par:HB * par + HB], den[0:T, i, HB * par:HB * par + HB]).then_inc(rden_made, 1)

            def probT_out(i):
                _, T, b = span(i)
                for par in range(2):
                    dve.wait_ge(flipped, 2 * i + par + 1)
                    if i >= 2:
                        dve.wait_ge(z_done, i - 1)
                    nc.vector.tensor_copy(probT[0:T, b, par, 0:HB * T], bank[4 + par][0:T, 0:HB * T]).then_inc(probT_made, 1)

            last_step = {"o": 1, "t": 2, "l": 3, "r": 4}

            def g_ready(what):
                if what in g_number:
                    dve.wait_ge(g_filled, g_number[what] + 1)
                else:
                    dve.wait_ge(last_filled, last_step[what[0]])

            def g_read(what, ins):
                if what in g_number:
                    ins.then_inc(g_evac, 1)
                    dve.wait_ge(g_evac, g_number[what] + 1)
                else:
                    ins.then_inc(last_evac, 1)
                    dve.wait_ge(last_evac, last_step[what[0]])

            def v_out(i):
                _, T, _ = span(i)
                g_ready(("v", i))
                if i >= 3:
                    dve.wait_ge(z_done, i - 2)
                nc.vector.tensor_copy(v_sb[0:T, i % 3, :], G[0:T, :]).then_inc(g_evac, 1)

            def z_lo_out(i):
                o, T, _ = span(i)
                dve.wait_ge(z_hi_made, i + 1)
                src = Z[:, 0:HB * T].rearrange("p (h n) -> p h n", h=HB)
                for t in range(o // P, (o + T - 1) // P + 1):
                    a, b = max(o, P * t), min(o + T, P * t + P)
                    hs = slice(HB * (i % 2), HB * (i % 2) + HB)
                    ins = nc.vector.tensor_tensor(zT_lo[:, t % 2, hs, a - P * t:b - P * t], src[:, :, a - o:b - o],
                                                  zT[:, hs, a:b].bitcast(F32), ALU.subtract)
                ins.then_inc(z_made, 1)

            def h2_of(t):
                r = rows_of[t]
                what = ("o", t)
                g_ready(what)
                dve.wait_ge(hx_made, t + 1)
                g_read(what, nc.vector.tensor_tensor(h_sb[0:r, t, :], h_sb[0:r, t, :], g_bank(what)[0:r, 0:D], ALU.add))
                chained(nc.vector.bn_stats(stats[0:r, 0, :], h_sb[0:r, t, :]))
                nc.vector.bn_aggr(mv[0:r, TILES + t, :], stats[0:r, 0, :]).then_inc(var_made, 1)

            def second_layernorm(t):
                r = rows_of[t]
                newton_step(TILES + t, r)
                layernorm(rec[0:r, t, 0, 0:D], h_sb[0:r, t, :], TILES + t, r).then_inc(rec_made, 1)

            def xn2T_out(t):
                r = rows_of[t]
                what = ("t", t)
                g_ready(what)
                g_read(what, nc.vector.tensor_copy(xn2T[:, 0:KD * r], g_bank(what)[:, 0:KD * r]))

            def logits_out(t):
                r = rows_of[t]
                what = ("l", t)
                g_ready(what)
                g_read(what, nc.vector.tensor_tensor(logits[0:r, :], g_bank(what)[0:r, 0:E], br_sb[0:r, :], ALU.add))

            def choose(t):
                r = rows_of[t]
                chained(nc.vector.max(top[0:r, :], logits[0:r, :]))
                nc.vector.tensor_tensor(gap[0:r, t:t + 1], top[0:r, 1:2], top[0:r, 0:1], ALU.subtract).then_inc(gap_made, 1)
                chained(nc.vector.max_index(topi[0:r, :], top[0:r, :], logits[0:r, :]))
                chained(nc.vector.tensor_copy(topf[0:r, :], topi[0:r, 0:2]))
                nc.vector.tensor_scalar(hot[0:r, t, 1, :], expert_no[0:r, :], topf[0:r, 1:2], None, ALU.is_equal)
                chained(nc.vector.tensor_scalar(hot[0:r, t, 0, :], expert_no[0:r, :], topf[0:r, 0:1], None, ALU.is_equal))
                nc.vector.tensor_tensor(chosen[0:r, t, :], hot[0:r, t, 0, :], hot[0:r, t, 1, :], ALU.add).then_inc(chosen_made, 1)
                chained(nc.vector.tensor_tensor(first_takes[0:r, t:t + 1], hot[0:r, t, 0, 0:1], hot[0:r, t, 1, 0:1], ALU.add))
                dve.wait_ge(chosen_made, t + 1)
                if t < last:
                    chained(nc.vector.tensor_tensor(chosen_sum[:, t + 1, :], chosen_sum[:, t, :], chosen[:, t, :], ALU.add))

            def first_gate(t):
                r = rows_of[t]
                dve.wait_ge(gsum_made, t + 1)
                nc.vector.reciprocal(rec[0:r, t, 0, D + 1:D + 2], gsum[0:r, t:t + 1]).then_inc(first_gate_made, 1)

            def ranks_out(t):
                r = rows_of[t]
                what = ("r", t)
                g_ready(what)
                rank = g_bank(what)[0:r, 0:E]
                nc.vector.tensor_scalar(at_slot[0:r, t, :], slot_no[0:r, :], rank[:, 0:1], first_takes[0:r, t:t + 1],
                                        ALU.is_equal, ALU.mult).then_inc(at_slot_made, 1)
                rank = rank.rearrange("p (a e) -> p a e", a=1).to_broadcast([r, 2, E])
                chained(nc.vector.tensor_tensor(where[0:r, :, :], rank, slot_base[0:r, t, :, :], ALU.add))
                g_read(what, nc.vector.scalar_tensor_tensor(out=kept[0:r, t, :, :], in0=rank, scalar=float(CAP), in1=where[0:r, :, :],
                                                            op0=ALU.is_lt, op1=ALU.mult))

            dve.wait_ge(small_in, 64)
            dve.wait_ge(slot_no_made, 1)
            dve.wait_ge(const_made, 1)
            v_out(0)
            row_max(0)
            for i in range(UNITS):
                if i < UNITS - 2:
                    row_rden(i)
                if i >= 5 and i % 2:
                    h2_of((i - 5) // 2)
                if i >= 7 and i % 2:
                    ranks_out((i - 7) // 2)
                if i >= 6 and i % 2 == 0 and i + 2 < UNITS:
                    logits_out((i - 6) // 2)
                if i + 1 < UNITS:
                    row_max(i + 1)
                if i + 2 == UNITS:
                    logits_out((i - 6) // 2)
                if i == UNITS - 1:
                    z_lo_out(i - 1)
                    probT_out(i)
                if i >= 5 and i % 2:
                    second_layernorm((i - 5) // 2)
                if 1 <= i < UNITS - 1 and i != UNITS - 3:
                    z_lo_out(i - 1)
                if i + 2 < UNITS and i % 2 == 0:
                    v_out(i + 2)
                if i < UNITS - 1:
                    probT_out(i)
                    if i == UNITS - 3:
                        z_lo_out(i - 1)
                        row_rden(i + 1)
                if i == UNITS - 1:
                    z_lo_out(i)
                if i >= 5 and i % 2:
                    xn2T_out((i - 5) // 2)
                if i >= 6 and i % 2 == 0:
                    choose((i - 6) // 2)
                if i == UNITS - 2:
                    row_rden(i + 1)
                if i >= 8 and i % 2 == 0:
                    first_gate((i - 8) // 2)
            first_gate(last - 2)
            logits_out(last - 1)
            choose(last - 1)
            h2_of(last)
            ranks_out(last - 1)
            second_layernorm(last)
            first_gate(last - 1)
            xn2T_out(last)
            logits_out(last)
            choose(last)
            ranks_out(last)
            first_gate(last)

            def slotT_out(e, b):
                dve.wait_ge(slotT_filled, e + 1)
                nc.vector.tensor_copy(slotT[:, b], bank[7][:, 0:KD * CAP].rearrange("p (k n) -> p k n", k=KD)).then_inc(slotT_made, 1)

            def outT_out(e, b, chunks=range(KD)):
                dve.wait_ge(out_filled, e + 1)
                for d in chunks:
                    ins = nc.vector.tensor_scalar(outT[:, b, d, :], bank[4 + d][:, 0:CAP],
                                                  biasT[:, bass.ds(E * MH + e * KD + d, 1)], None, ALU.add)
                ins.then_inc(outT_made, 1)

            def y_out(e, b, halves=range(2)):
                dve.wait_ge(y_filled, e + 1)
                nc.vector.tensor_copy(token[:, b, :], slot_meta[:, bass.ds(e, 1), :, 0:1].rearrange("p a s c -> p (a s c)").bitcast(U32))
                for s in halves:
                    ins = nc.vector.tensor_scalar(y_sb[:, b, s, :], bank[6][0:HALF, s * D:s * D + D],
                                                  slot_meta[:, bass.ds(e, 1), s, 1:2].rearrange("p a c -> p (a c)"), None, ALU.mult)
                ins.then_inc(y_made, 1)

            def mid(e, b):
                y_out(e - 1, 1 - b)
                slotT_out(e + 1, 1 - b)
                outT_out(e, b)

            slotT_out(1, 1)
            outT_out(0, 0)
            dve.wait_ge(meta_in, 16)
            mid(1, 1)
            mid(2, 0)
            with dve.Fori(3, E - 2, 2) as e:
                dve.wait_ge(added, 32 * (e - 2))
                mid(e, 1)
                dve.wait_ge(added, 32 * (e - 1))
                mid(e + 1, 0)
            dve.wait_ge(added, 32 * (E - 3))
            y_out(E - 2, 0)
            outT_out(E - 1, 1, [0])
            dve.wait_ge(added, 32 * (E - 2))
            y_out(E - 1, 1, [0])

        @block.tensor
        def _(pe):
            def free(i):
                j = use_before(uses[i][2], i)
                if j is not None:
                    s, v = emptied(j)
                    pe.wait_ge(s, v)

            def warm(n, spare):
                for _ in range(n):
                    pe.matmul(spare[:, 0:P], ident[:, :], ident[:, :], start=True, stop=True)

            pe.wait_ge(ident_made, 1)
            warm(9, bank[0])

            def transpose_channel(c):
                pe.wait_ge(sorted_act, c + 1)
                pe.wait_ge(sorted_dve, c + 1)
                for k in (2 * c, 2 * c + 1):
                    for part in range(2):
                        i = number["x", (k, part)]
                        free(i)
                        for w in range(3):
                            src = patches[:, c, 3 * part + w, P * (k % 2):P * (k % 2) + P]
                            mm = pe.transpose(bank_of[i][:, w * B * NPH:(w + 1) * B * NPH], src, ident[0:B * NPH, 0:B * NPH])
                        mm.then_inc(filled, 1)
                i = number["w", c]
                free(i)
                pe.wait_ge(w_in_in[c], 16)
                for k in (2 * c, 2 * c + 1):
                    for m in range(KD):
                        o = (k % 2) * D + m * P
                        mm = pe.transpose(bank_of[i][:, o:o + P], w_in[:, m, k * P:(k + 1) * P], ident[:, :])
                mm.then_inc(filled, 1)

            def embed(t, chunks):
                i, r = number["h", t], rows_of[t]
                for k in chunks:
                    pe.matmul(bank_of[i][0:r, 0:D], patchT[:, k, P * t:P * t + r], w_inT[:, k, :], start=(k == 0), stop=False)
                if k == KC - 1:
                    pe.matmul(bank_of[i][0:r, 0:D], spread_v[:, P * t:P * t + r], base_r[:, :], start=False, stop=True).then_inc(filled, 1)

            spread_v = spread[:, :, :].rearrange("s b t -> s (b t)")
            for c in range(C):
                transpose_channel(c)
                if c:
                    embed(HT, (2 * c - 2, 2 * c - 1))
                for i in (number["x", (2 * c + 1, 1)], number["w", c]):
                    s, v = emptied(i)
                    pe.wait_ge(s, v)
                if c == C - 1:
                    pe.wait_ge(base_made, 1)
                    pe.wait_ge(const_made, 1)
                for t in range(HT):
                    embed(t, (2 * c, 2 * c + 1))

            def flip_xn(t):
                i, r = number["xn", t], rows_of[t]
                free(i)
                pe.wait_ge(xn_made, t + 1)
                for k in range(KD):
                    mm = pe.transpose(bank_of[i][:, k * r:k * r + r], xn_sb[0:r, t, :].rearrange("p (m k) -> p k m", k=KD)[:, k, :], ident[0:r, 0:r])
                mm.then_inc(filled, 1)

            embed(HT, (KC - 2, KC - 1))
            embed(HT + 1, range(KC))
            for t in range(HT):
                flip_xn(t)
            i = number["bias", 0]
            free(i)
            pe.wait_ge(small_in, 64)
            pe.transpose(bank_of[i][:, 0:E * (MH + KD)], bias_rows[0:E * (MH + KD), :],
                         ident[0:E * (MH + KD), 0:E * (MH + KD)]).then_inc(filled, 1)

            def split_product(out_, lhs, rhs):
                terms = [(a, b, k) for a, b in SPLIT for k in range(KD)]
                for n, (a, b, k) in enumerate(terms):
                    mm = pe.matmul(out_, lhs[a](k), rhs[b](k), start=(n == 0), stop=(n == len(terms) - 1))
                return mm

            s, v = emptied(number["xn", HT - 1])
            pe.wait_ge(s, v)
            for half in range(2):
                for p in range(PAIRS):
                    for n, (name, w) in enumerate((("q", wq_r), ("k", wk_r))):
                        i = number[name, (p, half)]
                        free(i)
                        pe.wait_ge(split_lo, n + 1)
                        split_product(bank_of[i][:, 0:NH],
                                      [lambda k, part=part: part[:, k, 2 * DK * p:2 * DK * (p + 1)] for part in w],
                                      [lambda k, part=part: part[:, k, NH * half:NH * half + NH] for part in xnT]).then_inc(filled, 1)
                    if half == 0 and p in (1, 2):
                        flip_xn(HT + p - 1)
                if half == 0:
                    s, v = emptied(number["xn", TILES - 1])
                    pe.wait_ge(s, v)

            def g_free(what):
                if what in g_number:
                    if g_number[what]:
                        pe.wait_ge(g_evac, g_number[what])
                elif what[0] == "o":
                    pe.wait_ge(exped, 2 * UNITS)
                else:
                    pe.wait_ge(last_evac, "otlr".index(what[0]))

            def g_signal(what, mm):
                mm.then_inc(g_filled if what in g_number else last_filled, 1)

            def values(i):
                o, T, _ = span(i)
                g_free(("v", i))
                c = HU * DK * (i % 2)
                split_product(G[0:T, :], [lambda k, part=part: part[:, k, o:o + T] for part in xnT],
                              [lambda k, part=part: part[:, k, c:c + HU * DK] for part in wv_r]).then_inc(g_filled, 1)

            def scores(i, between=None):
                o, T, b = span(i)
                if i >= 2:
                    pe.wait_ge(exped, 2 * (i - 1))
                masked = T > S
                if masked:
                    for par in range(2):
                        lo = par * (P // 2)
                        pe.matmul(bank[2 * b + par][0:T, 0:HB * T], own[lo:lo + GB, :], other[lo:lo + GB, :],
                                  start=True, stop=False)
                for h in range(HB):
                    for par in range(2):
                        lo, p = par * (P // 2), HB * (i % 2) + h
                        mm = pe.matmul(bank[2 * b + par][0:T, h * T:h * T + T], qT[lo:lo + DK, p, o:o + T], kT[lo:lo + DK, p, o:o + T],
                                       start=not masked, stop=(h == HB - 1 or not masked))
                        if h == HB - 1:
                            mm.then_inc(scored, 1)
                    if h == HB // 2 - 1 and between:
                        between()

            def flip(i):
                _, T, b = span(i)
                for par in range(2):
                    pe.wait_ge(prob_made, 2 * i + par + 1)
                    if i >= 1:
                        pe.wait_ge(probT_made, 2 * (i - 1) + par + 1)
                    for h in range(HB):
                        mm = pe.transpose(bank[4 + par][0:T, h * T:h * T + T], prob[0:T, b, par, h * T:h * T + T], ident[0:T, 0:T])
                    mm.then_inc(flipped, 1)

            def weigh(i):
                _, T, b = span(i)
                pe.wait_ge(probT_made, 2 * i + 2)
                pe.wait_ge(g_evac, g_number["v", i] + 1)
                if i >= 1:
                    pe.wait_ge(z_made, i)
                for h in range(HB):
                    for par in range(2):
                        lo, c = par * (P // 2), (2 * h + par) * DK
                        mm = pe.matmul(Z[lo:lo + DK, h * T:h * T + T], v_sb[0:T, i % 3, c:c + DK], probT[0:T, b, par, h * T:h * T + T],
                                       start=True, stop=True)
                mm.then_inc(z_done, 1)

            def attention_out(t, between=None):
                r = rows_of[t]
                what = ("o", t)
                g_free(what)
                for p in range(PAIRS):
                    if p % HB == 0:
                        pe.wait_ge(z_made, min(2 * t + 4, UNITS) - 1 + p // HB)
                    z = (zT[:, p, P * t:P * t + r], zT_lo[:, t % 2, p, 0:r])
                    for a, b in SPLIT:
                        mm = pe.matmul(g_bank(what)[0:r, 0:D], z[a], wo_r[b][:, p, :], start=(p == 0 and a == b == 0),
                                       stop=(p == PAIRS - 1 and (a, b) == SPLIT[-1]))
                    for step in (between or {}).get(p, ()):
                        step()
                g_signal(what, mm)

            def flip_xn2(t):
                r = rows_of[t]
                what = ("t", t)
                g_free(what)
                pe.wait_ge(rec_made, t + 1)
                for k in range(KD):
                    mm = pe.transpose(g_bank(what)[:, k * r:k * r + r], rec[0:r, t, 0, k * P:(k + 1) * P], ident[0:r, 0:r])
                g_signal(what, mm)

            def router(t):
                r = rows_of[t]
                what = ("l", t)
                g_free(what)
                for k in range(KD):
                    mm = pe.matmul(g_bank(what)[0:r, 0:E], xn2T[:, k * r:k * r + r], wr_sb[:, k, :], start=(k == 0), stop=(k == KD - 1))
                g_signal(what, mm)

            def ranks(t):
                r = rows_of[t]
                what = ("r", t)
                g_free(what)
                dst = g_bank(what)[0:r, 0:E]
                pe.wait_ge(chosen_made, t + 1)
                pe.matmul(dst, before[0:r, 0:r], chosen[0:r, t, :], start=True, stop=False)
                g_signal(what, pe.matmul(dst, ones[:, 0:r], chosen_sum[:, t, :], start=False, stop=True))

            def dispatch(t):
                r = rows_of[t]
                pe.wait_ge(at_slot_made, t + 1)
                for k in range(KD):
                    mm = pe.matmul(bank[4 + k][:, 0:CAP], rec[0:r, t, 0, k * P:(k + 1) * P], at_slot[0:r, t, :],
                                   start=(t == 0), stop=(t == last))
                if t == last:
                    mm.then_inc(slotT_filled, 1)

            pe.wait_ge(split_lo, 4)
            s, v = emptied(use_before(7, len(uses)))
            pe.wait_ge(s, v)
            values(0)
            for name in ("q", "k"):
                s, v = emptied(number[name, (PAIRS - 1, 1)])
                pe.wait_ge(s, v)
            scores(0)
            values(1)
            for i in range(UNITS):
                routing = None
                if i >= 6 and i % 2 == 0:
                    routing = lambda: router((i - 6) // 2)
                if i >= 7 and i % 2:
                    routing = lambda: ranks((i - 7) // 2)
                if i + 1 < UNITS:
                    scores(i + 1, routing if i + 2 < UNITS else None)
                if i >= 1:
                    weigh(i - 1)
                if i + 2 >= UNITS:
                    routing()
                if i + 2 < UNITS:
                    values(i + 2)
                flip(i)
                if i >= 5 and i % 2 and i + 1 < UNITS:
                    flip_xn2((i - 5) // 2)
                if i >= 4 and i % 2 == 0:
                    attention_out((i - 4) // 2)
            pe.wait_ge(exped, 2 * UNITS)
            warm(4, bank[3])
            attention_out(last, {HB - 1: (lambda: weigh(UNITS - 1), lambda: flip_xn2(last - 1)),
                                 PAIRS - 3: (lambda: router(last - 1),)})
            pe.wait_ge(probT_made, 2 * UNITS)
            for t in range(last - 1):
                dispatch(t)
            ranks(last - 1)
            warm(12, Z)
            flip_xn2(last)
            warm(1, Z)
            router(last)
            dispatch(last - 1)
            warm(3, Z)
            ranks(last)
            warm(2, Z)
            dispatch(last)
            warm(2, Z)

            def flip_slots(e, b, n):
                pe.wait_ge(slots_in[b], 16 * n)
                for k in range(KD):
                    for s in range(2):
                        o = k * CAP + s * HALF
                        mm = pe.transpose(bank[7][:, o:o + HALF], slots[:, b, s, k * P:(k + 1) * P], ident[0:HALF, 0:HALF])
                mm.then_inc(slotT_filled, 1)

            def up(e, b, n, first_one=False):
                pe.wait_ge(w1_in[b], 16 * n)
                pe.wait_ge(slotT_made, e + 1)
                for m in range(MH):
                    j = m // 2
                    if m % 2 == 0 and not first_one:
                        pe.wait_ge(hid_made, MH // 2 * (e - 1) + j + 1)
                    for k in range(KD):
                        mm = pe.matmul(bank[j][:, (m % 2) * CAP:(m % 2) * CAP + CAP], w1_sb[:, b, k, m * P:(m + 1) * P], slotT[:, b, k, :],
                                       start=(k == 0), stop=(k == KD - 1))
                    if m % 2:
                        mm.then_inc(hid_filled, 1)

            def down(e, b, n, first_one=False, before_last=None):
                pe.wait_ge(w2_in[b], 16 * n)
                if not first_one:
                    pe.wait_ge(outT_made, e)
                for m in range(MH):
                    if m % 2 == 0:
                        pe.wait_ge(hid_made, MH // 2 * e + m // 2 + 1)
                    if m == MH - 1 and before_last:
                        before_last()
                    for d in range(KD):
                        mm = pe.matmul(bank[4 + d][:, 0:CAP], w2_sb[:, b, m, d * P:(d + 1) * P], hidT[:, b, m, :],
                                       start=(m == 0), stop=(m == MH - 1))
                mm.then_inc(out_filled, 1)

            def flip_out(e, b):
                pe.wait_ge(outT_made, e + 1)
                for s in range(2):
                    for d in range(KD):
                        o = s * D + d * P
                        mm = pe.transpose(bank[6][0:HALF, o:o + P], outT[:, b, d, s * HALF:(s + 1) * HALF], ident[:, :])
                mm.then_inc(y_filled, 1)

            def expert(e, b, n, n_next, first_rows=False):
                up(e, b, n)
                if not first_rows:
                    pe.wait_ge(y_made, e - 1)
                flip_out(e - 1, 1 - b)
                flip_slots(e + 1, 1 - b, n_next)
                down(e, b, n)

            pe.wait_ge(g_evac, len(g_uses))
            pe.wait_ge(last_evac, 4)
            up(0, 0, 1, first_one=True)
            down(0, 0, 1, first_one=True, before_last=lambda: flip_slots(1, 1, 1))
            expert(1, 1, 1, 1, first_rows=True)
            with pe.Fori(2, E - 3, 2) as e:
                expert(e, 0, (e >> 1) + 1, (e >> 1) + 1)
                expert(e + 1, 1, (e >> 1) + 1, (e >> 1) + 1)
            expert(E - 2, 0, E // 2, E // 2)
            up(E - 1, 1, E // 2)
            pe.wait_ge(y_made, E - 2)
            flip_out(E - 2, 0)
            down(E - 1, 1, E // 2)
            pe.wait_ge(y_made, E - 1)
            pe.wait_ge(outT_made, E)
            pe.wait_ge(outT_half_made, 1)
            for s, (dst, done) in enumerate(((bank[6], y_filled), (bank[7], y_half_filled))):
                for d in range(KD):
                    mm = pe.transpose(dst[0:HALF, d * P:d * P + P], outT[:, 1, d, s * HALF:(s + 1) * HALF], ident[:, :])
                mm.then_inc(done, 1)


_INS = ["x", "cls_tok", "L0_tok_W", "L0_tok_b", "L0_tok_cls_token", "L0_tok_pos_embed", "L0_attn_w_q", "L0_attn_w_k",
        "L0_attn_w_v", "L0_attn_w_o", "L0_ffn_Wr", "L0_ffn_br", "L0_ffn_W1", "L0_ffn_b1", "L0_ffn_W2", "L0_ffn_b2"]


def kernel(**inputs):
    import numpy as _np
    import concourse.bacc as _bacc
    from concourse import mybir as _mybir
    from concourse.bass_utils import run_bass_kernel_spmd as _run

    nc = _bacc.Bacc("TRN2", target_bir_lowering=False, num_devices=1)
    arrays, args = {}, []
    for name in _INS:
        a = _np.ascontiguousarray(inputs[name])
        arrays[f"in_{name}_dram"] = a
        args.append(nc.dram_tensor(f"in_{name}_dram", a.shape, _mybir.dt.from_np(a.dtype), kind="ExternalInput").ap())
    images = inputs["x"].shape[0]
    tokens = inputs["L0_tok_pos_embed"].shape[1] + 1
    experts = inputs["L0_ffn_W1"].shape[0]
    dim = inputs["cls_tok"].shape[2]
    n = images * tokens
    out = nc.dram_tensor("out_0_dram", (n + n * 2 // experts, dim), _mybir.dt.float32, kind="ExternalOutput").ap()
    vit_block(nc, *args, out)
    r = _run(nc, [arrays], core_ids=[0])
    return r.results[0]["out_0_dram"][:n].reshape(images, tokens, dim)
```
